# Optimizing a Trainium2 kernel written in Bass

```python
import numpy as np
import jax
import jax.numpy as jnp

def _softmax(x, axis=-1):
    return jax.nn.softmax(x, axis=axis)

def _gelu(x):
    return jax.nn.gelu(x, approximate=True)

def _silu(x):
    return jax.nn.silu(x)

def _sigmoid(x):
    return jax.nn.sigmoid(x)

def _layernorm(x, axis=-1, eps=1e-05):
    m = jnp.mean(x, axis=axis, keepdims=True)
    v = jnp.var(x, axis=axis, keepdims=True)
    return (x - m) / jnp.sqrt(v + eps)

def _scatter_add(tgt, idx, src, axis=0):
    return tgt.at[idx].add(src)

def _segment_sum(src, seg, n):
    return jax.ops.segment_sum(src, seg, n)
kernel_name = 'mk_metaformer_d1_conv_nchw384_r2_755444'

def setup_inputs(seed: int=0):
    np.random.seed(seed)
    _w = jnp.asarray

    def _rec_inputs():
        import jax
        import jax.numpy as jnp
        _gk = jax.random.key(seed)
        x = -0.0002221 + 1 * jax.random.normal(jax.random.fold_in(_gk, 1), (16, 192, 32, 32), jnp.float32)
        return x
    x = _rec_inputs()

    def _L0_conv_setup():
        import jax, jax.numpy as jnp
        import numpy as np
        STRIDE = 1
        PAD = 3

        def _dwconv(x, w, stride, pad):
            C = x.shape[1]
            return jax.lax.conv_general_dilated(x, w, window_strides=(stride, stride), padding=[(pad, pad), (pad, pad)], dimension_numbers=('NCHW', 'OIHW', 'NCHW'), feature_group_count=C)
        key = jax.random.key(seed)
        k1, k2 = jax.random.split(key)
        x = jax.random.normal(k1, (16, 192, 32, 32), dtype=jnp.float32)
        k_sz = 7
        fan_out = 1 * k_sz * k_sz
        std = np.sqrt(2.0 / fan_out).astype(np.float32)
        weight = jax.random.normal(k2, (192, 1, k_sz, k_sz), dtype=jnp.float32) * std
        return {'x': x, 'weight': weight}
    _L0_conv_all = _L0_conv_setup()
    _L0_conv_in = {k: v for k, v in _L0_conv_all.items() if k in ('weight',)}
    del _L0_conv_all

    def _L0_ffn_setup():
        import jax, jax.numpy as jnp
        import numpy as np
        NUM_GROUPS = 5
        EPS = 1e-05
        QB = 128.0

        def _binarize_weights_groupwise(W):
            n_out = W.shape[0]
            gs = n_out // NUM_GROUPS
            Wb = jnp.zeros_like(W)
            for g in range(NUM_GROUPS):
                wg = W[g * gs:(g + 1) * gs]
                z = wg - wg.mean()
                ste = z + jax.lax.stop_gradient(jnp.sign(z) - z)
                Wb = Wb.at[g * gs:(g + 1) * gs].set(ste)
            return Wb

        def _quantize_activations_groupwise(x):
            n = x.shape[0]
            gs = n // NUM_GROUPS
            xq = jnp.zeros_like(x)
            for g in range(NUM_GROUPS):
                ag = x[g * gs:(g + 1) * gs]
                gamma = jnp.max(jnp.abs(ag))
                xq = xq.at[g * gs:(g + 1) * gs].set(jnp.clip(ag * QB / (gamma + EPS), -QB + EPS, QB - EPS))
            return xq

        def _bitlinear(x, W, b):
            Wb = _binarize_weights_groupwise(W)
            y = jnp.einsum('btc,oc->bto', x, Wb) + b
            return _quantize_activations_groupwise(y)
        key = jax.random.key(seed)
        k1, k2, k3, k4, k5 = jax.random.split(key, 5)
        B, T, C = (10, 1024, 192)
        H = 4 * C
        lim1 = 1.0 / np.sqrt(C)
        lim2 = 1.0 / np.sqrt(H)
        x = jax.random.normal(k1, (B, T, C), dtype=jnp.float32)
        W1 = jax.random.uniform(k2, (H, C), minval=-lim1, maxval=lim1, dtype=jnp.float32)
        b1 = jax.random.uniform(k3, (H,), minval=-lim1, maxval=lim1, dtype=jnp.float32)
        W2 = jax.random.uniform(k4, (C, H), minval=-lim2, maxval=lim2, dtype=jnp.float32)
        b2 = jax.random.uniform(k5, (C,), minval=-lim2, maxval=lim2, dtype=jnp.float32)
        return {'x': x, 'W1': W1, 'b1': b1, 'W2': W2, 'b2': b2}
    _L0_ffn_all = _L0_ffn_setup()
    _L0_ffn_in = {k: v for k, v in _L0_ffn_all.items() if k in ('W1', 'b1', 'W2', 'b2')}
    del _L0_ffn_all
    return {'x': x, 'L0_conv_weight': _L0_conv_in['weight'], 'L0_ffn_W1': _L0_ffn_in['W1'], 'L0_ffn_b1': _L0_ffn_in['b1'], 'L0_ffn_W2': _L0_ffn_in['W2'], 'L0_ffn_b2': _L0_ffn_in['b2']}

def reference(x, L0_conv_weight, L0_ffn_W1, L0_ffn_b1, L0_ffn_W2, L0_ffn_b2):
    import jax
    import jax.numpy as jnp

    def _L0_conv_ref(x, weight):
        import jax, jax.numpy as jnp
        import numpy as np
        STRIDE = 1
        PAD = 3

        def _dwconv(x, w, stride, pad):
            C = x.shape[1]
            return jax.lax.conv_general_dilated(x, w, window_strides=(stride, stride), padding=[(pad, pad), (pad, pad)], dimension_numbers=('NCHW', 'OIHW', 'NCHW'), feature_group_count=C)
        w_sym = (weight + jnp.rot90(weight, k=1, axes=(2, 3)) + jnp.rot90(weight, k=2, axes=(2, 3)) + jnp.rot90(weight, k=3, axes=(2, 3))) * 0.25
        return _dwconv(x, w_sym, STRIDE, PAD)

    def _L0_ffn_ref(x, W1, b1, W2, b2):
        import jax, jax.numpy as jnp
        import numpy as np
        NUM_GROUPS = 5
        EPS = 1e-05
        QB = 128.0

        def _binarize_weights_groupwise(W):
            n_out = W.shape[0]
            gs = n_out // NUM_GROUPS
            Wb = jnp.zeros_like(W)
            for g in range(NUM_GROUPS):
                wg = W[g * gs:(g + 1) * gs]
                z = wg - wg.mean()
                ste = z + jax.lax.stop_gradient(jnp.sign(z) - z)
                Wb = Wb.at[g * gs:(g + 1) * gs].set(ste)
            return Wb

        def _quantize_activations_groupwise(x):
            n = x.shape[0]
            gs = n // NUM_GROUPS
            xq = jnp.zeros_like(x)
            for g in range(NUM_GROUPS):
                ag = x[g * gs:(g + 1) * gs]
                gamma = jnp.max(jnp.abs(ag))
                xq = xq.at[g * gs:(g + 1) * gs].set(jnp.clip(ag * QB / (gamma + EPS), -QB + EPS, QB - EPS))
            return xq

        def _bitlinear(x, W, b):
            Wb = _binarize_weights_groupwise(W)
            y = jnp.einsum('btc,oc->bto', x, Wb) + b
            return _quantize_activations_groupwise(y)
        h = _bitlinear(x, W1, b1)
        h = jax.nn.gelu(h, approximate=False)
        out = _bitlinear(h, W2, b2)
        return out

    def _gn(v, G=32, eps=1e-05):
        B_, C_, H_, W_ = v.shape
        g = v.reshape(B_, G, C_ // G, H_, W_)
        m = jnp.mean(g, axis=(2, 3, 4), keepdims=True)
        s = jnp.var(g, axis=(2, 3, 4), keepdims=True)
        return ((g - m) / jnp.sqrt(s + eps)).reshape(v.shape)

    def _ln_c(v, eps=1e-06):
        m = jnp.mean(v, axis=1, keepdims=True)
        s = jnp.var(v, axis=1, keepdims=True)
        return (v - m) / jnp.sqrt(s + eps)

    def _ln_t(v, eps=1e-05):
        m = jnp.mean(v, axis=-1, keepdims=True)
        s = jnp.var(v, axis=-1, keepdims=True)
        return (v - m) / jnp.sqrt(s + eps)

    def _to_tokens(v):
        B_, C_, H_, W_ = v.shape
        return v.reshape(B_, C_, H_ * W_).transpose(0, 2, 1)

    def _from_tokens(t, like):
        B_, C_, H_, W_ = like.shape
        return t.transpose(0, 2, 1).reshape(B_, C_, H_, W_)
    x = x + _L0_conv_ref(_ln_c(x), L0_conv_weight)
    t = _to_tokens(x)
    t = t + _L0_ffn_ref(_ln_t(t), L0_ffn_W1, L0_ffn_b1, L0_ffn_W2, L0_ffn_b2)
    x = _from_tokens(t, x)
    return x

_drawn_inputs = setup_inputs


def setup_inputs(seed=0):
    import zlib

    import numpy as np

    out = dict(_drawn_inputs(seed))
    spreads = {}
    factors = {'L0_ffn_b1': 8.0, 'L0_ffn_b2': 8.0}
    for name, (base, spread) in spreads.items():
        noise = np.random.default_rng([zlib.crc32(name.encode()), seed]).standard_normal(out[name].shape)
        drawn = base * np.exp(spread * noise) if base else spread * noise
        out[name] = jnp.asarray(drawn.astype(out[name].dtype))
    for name, factor in factors.items():
        out[name] = (out[name] * factor).astype(out[name].dtype)
    return out
```

```python
import concourse.bass as bass
from concourse import mybir
from contextlib import ExitStack

F32 = mybir.dt.float32
F16 = mybir.dt.float16
ALU = mybir.AluOpType
ACT = mybir.ActivationFunctionType
AX = mybir.AxisListType

P = 128
B, C, H, W = 16, 192, 32, 32
PIX = H * W
HID = 4 * C
KS, PAD = 7, 3
GROUPS = 5
C1 = C - P
PAIRS = B // 2
CHUNK = PAIRS // 2
QW = 32
HALF = PIX // 2
HROWS = H // 2
TILES = B
TW = 3 * HALF
NST = 3 * HROWS
XSC, WSC = 16.0, 256.0
RMAX = bass.bass_isa.ReduceOp.max
QB, QEPS = 128.0, 1e-5
CLIP = 127.99999237060547
HSC = 256.0
MT = HID // P
FT = (B // GROUPS * GROUPS) * 2
GT = FT // GROUPS
YR, Y2R = 10, 8
LAG2 = 8
LAGA = LAG2 - 1
LAGE = LAG2 + 1
LAGF = 2 * LAG2
RW = 64
KP = 2 * KS


def build(nc, x, cw, w1, b1, w2, b2, out):
    ctx = ExitStack()
    with ctx:
        arena = ctx.enter_context(nc.sbuf_tensor("arena", [P, 50304], F32))

        def view(at, words, dt=F32):
            v = arena[:, at:at + words]
            return v if dt == F32 else v.bitcast(dt)

        def sb(name, shape, dt=F32):
            return ctx.enter_context(nc.sbuf_tensor(name, shape, dt))

        def sem(name):
            return ctx.enter_context(nc.semaphore(name))

        ker_d = nc.dram_tensor("ker_d", (C, RW, KP), F16)
        band_d = nc.dram_tensor("band_d", (C, QW, QW * KP), F16)
        x1_d = nc.dram_tensor("x1_d", (B, C, PIX), F32)
        tn_d = nc.dram_tensor("tn_d", (B, C, PIX), F32)
        ker_d, band_d, x1_d, tn_d = (t.ap() for t in (ker_d, band_d, x1_d, tn_d))

        XB = view(0, 24576).rearrange("p (k s n) -> p k s n", k=PAIRS, s=3)
        STG = view(24576, 6144).rearrange("p (r s n) -> p r s n", r=4, s=3)
        DV = view(30720, 3072).rearrange("p (r s n) -> p r s n", r=2, s=3)
        XH = view(33792, 6144, F16).rearrange("p (k s h i) -> p k s h i", k=CHUNK, s=3, h=H)
        XL = view(39936, 6144, F16).rearrange("p (k s h i) -> p k s h i", k=CHUNK, s=3, h=H)
        BD = view(46080, 3584, F16).rearrange("p (g r c k) -> p g r c k", g=2, r=2, c=P)
        w1f = view(33792, 2880).rearrange("p (g n) -> p g n", g=GROUPS)
        w1s = view(36672, 1440, F16).rearrange("p (g r c) -> p g r c", g=GROUPS, r=3)
        w2f = view(38112, 3840).rearrange("p (g n) -> p g n", g=GROUPS)
        w2s = view(41952, 1920, F16).rearrange("p (g m f) -> p g m f", g=GROUPS, m=MT)
        kraw = view(46080, 98).rearrange("p (s a b) -> p s a b", s=2, a=KS)
        kacc = view(46180, 98).rearrange("p (s a b) -> p s a b", s=2, a=KS)
        kpad = view(46280, 896, F16).rearrange("p (s t k) -> p s t k", s=2, t=RW)
        Y = view(0, YR * MT * HALF).rearrange("p (r m n) -> p r m n", r=YR, m=MT)
        at = YR * MT * HALF
        Y2 = view(at, Y2R * 2 * HALF).rearrange("p (r s n) -> p r s n", r=Y2R, s=2)
        at += Y2R * 2 * HALF
        TAW = view(at, 2 * HALF).rearrange("p (r n) -> p r n", r=2)
        TA = view(at, 2 * HALF, F16).rearrange("p (r n) -> p r n", r=2)
        at += 2 * HALF
        TB = view(at, 2 * (HALF + 1), F16).rearrange("p (r n) -> p r n", r=2)
        at += 2 * (HALF + 1) + 2
        HI = view(at, MT * HALF, F16).rearrange("p (r m n) -> p r m n", r=2, m=MT)
        at += MT * HALF
        XO = view(at, 4 * HALF).rearrange("p (r s n) -> p r s n", r=2, s=2)
        at += 4 * HALF
        assert at <= 50304

        sumlo = sb("sumlo", [P, P])
        sumhi = sb("sumhi", [P, P])
        sumall = sb("sumall", [P, P])
        ones = sb("ones", [P, P])
        ident = sb("ident", [P, P], F16)
        W1A = sb("W1A", [P, HID], F16)
        W1B = sb("W1B", [P, HID], F16)
        W2T = sb("W2T", [P, MT, C], F16)
        b1s = sb("b1s", [P, MT])
        b2s = sb("b2s", [P, 2])
        eps = sb("eps", [P, 2])
        S1 = sb("S1", [P, 2, NST])
        S2 = sb("S2", [P, 2, NST])
        MU = sb("MU", [P, 2, NST])
        SD = sb("SD", [P, 2, NST])
        RS = sb("RS", [P, 2, NST])
        wsum = sb("wsum", [P, 2 * GROUPS])
        wmean = sb("wmean", [P, 2 * GROUPS])
        am = sb("am", [P, GT])
        am2 = sb("am2", [P, GT * 2])
        gm = sb("gm", [P, 8])

        bank = [ctx.enter_context(nc.psum_tensor(f"bank{i}", [P, 512], F32)) for i in range(5)]
        sqp = ctx.enter_context(nc.psum_tensor("sqp", [P, TW], F32))
        cps = [[bank[0], bank[1]], [bank[2], bank[3]]]
        stp = bank[4]
        m1p = [bank[0], bank[1], bank[2], bank[3]]
        m2p = [[bank[4][:, :], sqp[:, 0:512]], [sqp[:, 512:1024], sqp[:, 1024:1536]]]

        t1a = bank[0][:, 0:480].bitcast(F16)
        t1b = bank[1][:, 0:480].bitcast(F16)
        t2 = [bank[2 + m // 3][:, (m % 3) * 96:(m % 3) * 96 + 95].bitcast(F16).rearrange("p (g q) -> p g q", g=GROUPS)
              for m in range(MT)]

        ld_w = sem("ld_w"); ld_k = sem("ld_k"); ld_b = sem("ld_b")
        ld_x = [sem(f"ld_x{i}") for i in range(4)]
        ld_band = [[sem(f"ld_band{g}{r}") for r in range(2)] for g in range(2)]
        st_ker = sem("st_ker"); st_band = sem("st_band")
        st_x1 = [sem(f"st_x1{i}") for i in range(2)]
        st_tn = [sem(f"st_tn{i}") for i in range(2)]
        consts = sem("consts")
        prep_sum = sem("prep_sum"); prep_tot = sem("prep_tot"); prep_mean = sem("prep_mean")
        prep_sign = sem("prep_sign"); prep_t = sem("prep_t"); prep_done = sem("prep_done")
        ker_step = sem("ker_step"); bias_step = sem("bias_step"); zeroed = sem("zeroed")
        names = "xb s1 mps mu d sq s2 vps sd r xn hi lo xt tt"
        ln = [{n: sem(f"ln{p}_{n}") for n in names.split()} for p in range(2)]
        conv = [sem("conv0"), sem("conv1")]
        cadd = [sem("cadd0"), sem("cadd1")]
        ld_ta = [sem(f"ld_ta{i}") for i in range(2)]
        ld_xo = [sem(f"ld_xo{i}") for i in range(2)]
        st_o = [sem(f"st_o{i}") for i in range(2)]
        st_tail = sem("st_tail")
        mm1 = sem("mm1"); ev1 = sem("ev1"); mm2 = [sem("mm2a"), sem("mm2b")]; ev2 = sem("ev2")
        amx = sem("amx"); amx2 = sem("amx2"); gmx = sem("gmx"); gall = sem("gall"); gsc_t = sem("gsc_t"); gsc = sem("gsc")
        gmx2 = sem("gmx2"); gall2 = sem("gall2"); gsc2_t = sem("gsc2_t"); gsc2 = sem("gsc2")
        gelu = sem("gelu"); hs = sem("hs"); hi2 = sem("hi2"); lo2 = sem("lo2")
        clipd = sem("clipd"); fin = sem("fin")

        block = ctx.enter_context(nc.Block())

        def xslab(t, dram):
            k, cols = t // 2, slice((t % 2) * HALF, (t % 2 + 1) * HALF)
            return (dram[2 * k:2 * k + 2, 0:P, cols].rearrange("b c n -> c b n"),
                    dram[2 * k, P:C, cols], dram[2 * k + 1, P:C, cols])

        def xtile(t):
            return XB[:, t // 2, :, (t % 2) * HALF:(t % 2 + 1) * HALF]

        def rows(v):
            return v.rearrange("p s (h i) -> p s h i", i=32)

        def per_row(v, par):
            return v[:, par, :].rearrange("p (s h) -> p s h", s=3).unsqueeze(3).to_broadcast([P, 3, HROWS, 32])

        def tap(g, dh):
            lo, hi = max(0, -dh), min(H, H - dh)
            sl = slice(0, 2) if g == 0 else slice(2, 3)
            return lo, hi, sl

        @block.sync
        def _(sp):
            sp.dma_start(kraw[:, 0, :, :], cw[0:P, 0, :, :]).then_inc(ld_k, 16)
            sp.dma_start(kraw[0:C1, 1, :, :], cw[P:C, 0, :, :]).then_inc(ld_k, 16)
            rp1, rp2 = HID // GROUPS // 3, C // GROUPS
            for g in range(GROUPS):
                sp.dma_start(w1f[0:rp1, g, :], w1[g * 3 * rp1:(g + 1) * 3 * rp1, :]
                             .rearrange("(p r) c -> p (r c)", r=3)).then_inc(ld_w, 16)
                sp.dma_start(w2f[0:rp2, g, :], w2[g * rp2:(g + 1) * rp2, :]).then_inc(ld_w, 16)
            sp.dma_start(b1s[:, :], b1.rearrange("(m p) -> p m", p=P), allow_slow_non_contiguous=True).then_inc(ld_b, 16)
            sp.dma_start(b2s[:, 0:1], b2[0:P].rearrange("(p o) -> p o", o=1)).then_inc(ld_b, 16)
            sp.dma_start(b2s[0:C1, 1:2], b2[P:C].rearrange("(p o) -> p o", o=1)).then_inc(ld_b, 16)

            def load_x(t):
                if t >= 4:
                    sp.wait_ge(ln[0]["s2"], t - 3)
                a, lo, hi = xslab(t, x)
                sp.dma_start(STG[:, t % 4, 0:2, :], a).then_inc(ld_x[t % 4], 16)
                sp.dma_start(STG[0:C1, t % 4, 2, :], lo).then_inc(ld_x[t % 4], 16)
                sp.dma_start(STG[C1:P, t % 4, 2, :], hi).then_inc(ld_x[t % 4], 16)

            def load_band(i, r, done):
                for g in range(2):
                    if done is not None:
                        sp.wait_ge(conv[g], done)
                    for q in range(4):
                        c = (q if g == 0 else 4 + q % 2) * 32 + i
                        src = band_d[bass.ds(c, 1), :, :].rearrange("o w n -> (o w) n")
                        sp.dma_start(BD[q * QW:(q + 1) * QW, g, r, q * QW:(q + 1) * QW, :], src) \
                            .then_inc(ld_band[g][r], 16)

            for t in range(4):
                load_x(t)
            sp.wait_ge(ker_step, 9)
            sp.dma_start(ker_d[0:P, :, :], kpad[:, 0, :, :]).then_inc(st_ker, 16)
            sp.dma_start(ker_d[P:C, :, :], kpad[0:C1, 1, :, :]).then_inc(st_ker, 16)
            sp.wait_ge(st_ker, 32)
            for n in range(4):
                c0, nc_ = n * (C // 4), C // 4
                src = bass.AP(ker_d.tensor, c0 * RW * KP + (QW - 1) * KP, [[RW * KP, nc_], [-KP, QW], [1, QW * KP]])
                sp.dma_start(band_d[c0:c0 + nc_, :, :], src).then_inc(st_band, 16)
            sp.wait_ge(st_band, 64)
            sp.wait_ge(zeroed, 1)
            load_band(0, 0, None)
            load_band(1, 1, None)
            for t in range(4, 12):
                load_x(t)
            with sp.Fori(1, 16) as m:
                load_band(2 * m, 0, 2 * m - 1)
                load_band(2 * m + 1, 1, 2 * m)
            for t in range(12, TILES):
                load_x(t)
            with sp.Fori(16, 32) as m:
                load_band((m - 16) * 2, 0, 2 * m - 1)
                load_band((m - 16) * 2 + 1, 1, 2 * m)

            def load_tokens(s):
                b, half, cols = s // 2, s % 2, slice((s % 2) * HALF, (s % 2 + 1) * HALF)
                sp.wait_ge(st_tn[half], 48 * (b // 2 + 1))
                if s >= 2:
                    sp.wait_ge(mm1, MT * (s - 1))
                sp.dma_start(TAW[:, s % 2, :], tn_d[b, 0:P, cols]).then_inc(ld_ta[s % 2], 16)
                src = tn_d[b, P:C, cols].bitcast(F16)
                sp.dma_start(TB[0:C1, s % 2, 1:1 + 2 * HALF], src).then_inc(ld_ta[s % 2], 16)
                sp.dma_start(TB[C1:P, s % 2, 0:2 * HALF], src).then_inc(ld_ta[s % 2], 16)

            def load_x1(u):
                b, half, cols = u // 2, u % 2, slice((u % 2) * HALF, (u % 2 + 1) * HALF)
                sp.wait_ge(st_x1[half], 48 * (b // 2 + 1))
                if u >= 2:
                    sp.wait_ge(st_o[u % 2], 32 * (u // 2))
                sp.dma_start(XO[:, u % 2, 0, :], x1_d[b, 0:P, cols]).then_inc(ld_xo[u % 2], 16)
                sp.dma_start(XO[0:C1, u % 2, 1, :], x1_d[b, P:C, cols]).then_inc(ld_xo[u % 2], 16)

            def store(u):
                b, cols = u // 2, slice((u % 2) * HALF, (u % 2 + 1) * HALF)
                sp.wait_ge(fin, 2 * u + 2)
                sp.dma_start(out[b, 0:P, cols], XO[:, u % 2, 0, :]).then_inc(st_o[u % 2], 16)
                sp.dma_start(out[b, P:C, cols], XO[0:C1, u % 2, 1, :]).then_inc(st_o[u % 2], 16)

            for g in range(2):
                sp.wait_ge(conv[g], 64)
            load_tokens(0)
            load_tokens(1)
            for s in range(FT + LAGF + 1):
                if s + 2 < FT:
                    load_tokens(s + 2)
                if 0 <= s - LAGF - 1 < FT:
                    store(s - LAGF - 1)
                if 0 <= s - LAGF + 1 < FT:
                    load_x1(s - LAGF + 1)
            for e in range(2):
                sp.wait_ge(st_x1[e], 48 * PAIRS)
            sp.dma_start(out[B - 1, :, :], x1_d[B - 1, :, :]).then_inc(st_tail, 16)
            sp.wait_ge(st_tail, 16)
            for e in range(2):
                sp.wait_ge(st_o[e], 32 * (FT // 2))
                sp.wait_ge(st_tn[e], 48 * PAIRS)

        @block.gpsimd
        def _(pool):
            pool.memset(ident[:, :], 0.0).then_inc(consts, 1)
            pool.memset(sumlo[:, :], 0.0).then_inc(consts, 1)
            pool.memset(sumhi[:, :], 0.0).then_inc(consts, 1)
            pool.memset(sumall[:, :], 0.0).then_inc(consts, 1)
            pool.memset(ones[:, :], 1.0).then_inc(consts, 1)
            pool.memset(eps[:, 0:1], 1e-6 / (XSC * XSC)).then_inc(consts, 1)
            pool.memset(eps[:, 1:2], 1e-5 / (XSC * XSC)).then_inc(consts, 1)
            n = 7
            pool.wait_ge(consts, n)
            pool.affine_select(out=ident[:, :], in_=ident[:, :], compare_op=ALU.not_equal, fill=1.0, base=0,
                               pattern=[[-1, P]], channel_multiplier=1).then_inc(consts, 1)
            n += 1
            for q in range(4):
                for m in (sumall, sumlo if q < 2 else sumhi):
                    v = m[:, :].rearrange("p (a b) -> p a b", b=QW)
                    pool.affine_select(out=v, in_=v, compare_op=ALU.not_equal, fill=1.0, base=-q * QW,
                                       pattern=[[0, 4], [-1, QW]], channel_multiplier=1).then_inc(consts, 1)
                    n += 1
                    pool.wait_ge(consts, n)

            def scale(p, t):
                pool.wait_ge(ln[p]["r"], t + 1)
                v = rows(DV[:, t % 2, :, :])
                pool.tensor_tensor(out=v, in0=v, in1=per_row(RS, t % 2), op=ALU.mult).then_inc(ln[p]["xn"], 1)

            for t in range(TILES):
                scale(0, t)
            for t in range(TILES):
                scale(1, t)
            for s in range(FT + LAGF):
                u = s - LAGA
                if 0 <= u < FT:
                    pool.wait_ge(hi2, u + 1)
                    yv = Y[:, u % YR, :, :]
                    lov = yv.bitcast(F16).rearrange("p m (n e) -> p m n e", e=2)[:, :, :, 0]
                    pool.tensor_tensor(out=lov, in0=yv, in1=HI[:, u % 2, :, :], op=ALU.subtract).then_inc(lo2, 1)
                if 1 <= s <= FT and s % GT == 0:
                    g = s // GT - 1
                    pool.wait_ge(gmx, g + 1)
                    pool.partition_all_reduce(gm[:, 1:2], gm[:, 0:1], P, RMAX).then_inc(gall, 1)
                u = s - LAGE
                if 0 <= u < FT and u % GT == GT - 1:
                    g = u // GT
                    pool.wait_ge(gmx2, g + 1)
                    pool.partition_all_reduce(gm[:, 5:6], gm[:, 4:5], P, RMAX).then_inc(gall2, 1)

        @block.scalar
        def _(act):
            act.wait_ge(prep_mean, 1)
            rp1, rp2 = HID // GROUPS // 3, C // GROUPS
            for g in range(GROUPS):
                act.activation(w1s[0:rp1, g, :, :], w1f[0:rp1, g, :].rearrange("p (r c) -> p r c", r=3), ACT.Sign,
                               bias=wmean[0:rp1, g:g + 1], scale=1.0).then_inc(prep_sign, 1)
                act.activation(w2s[0:rp2, g, :, :], w2f[0:rp2, g, :].rearrange("p (m f) -> p m f", m=MT), ACT.Sign,
                               bias=wmean[0:rp2, GROUPS + g:GROUPS + g + 1], scale=1.0).then_inc(prep_sign, 1)

            def stat(dst, src, **kw):
                func = kw.pop("func")
                bias = kw.pop("bias", None)
                def go(o, i, lo, hi):
                    b = {} if bias is None else {"bias": bias[lo:hi, :]}
                    return act.activation(o, i, func, **b, **kw)
                go(dst[:, 0:2 * HROWS], src[:, 0:2 * HROWS], 0, P)
                go(dst[0:C1, 2 * HROWS:NST], src[0:C1, 0:HROWS], 0, C1)
                return go(dst[C1:P, 2 * HROWS:NST], src[C1:P, HROWS:2 * HROWS], C1, P)

            def ln_step(p, t, n0, first=0):
                L = ln[p]
                if t < n0:
                    act.wait_ge(L["mps"], t + 1)
                    stat(MU[:, t % 2, :], stp[:, (t % 2) * 32:(t % 2) * 32 + 32], func=ACT.Copy, scale=1.0 / C) \
                        .then_inc(L["mu"], 1)
                if t >= first + 1:
                    act.wait_ge(L["vps"], t)
                    u = t - 1
                    stat(SD[:, u % 2, :], stp[:, 64 + (u % 2) * 32:96 + (u % 2) * 32], func=ACT.Sqrt,
                         bias=eps[:, p:p + 1], scale=1.0 / (C * XSC * XSC)).then_inc(L["sd"], 1)
                if t < n0:
                    act.wait_ge(L["d"], t + 1)
                    if t >= 1:
                        act.wait_ge(L["s2"], t)
                    act.activation(sqp[:, :].rearrange("p (s n) -> p s n", s=3), DV[:, t % 2, :, :], ACT.Square) \
                        .then_inc(L["sq"], 1)
                if t >= first + 1:
                    u = t - 1
                    act.wait_ge(L["xn"], u + 1)
                    if p == 0:
                        if u == TILES // 2:
                            act.wait_ge(conv[1], 32)
                            act.wait_ge(conv[0], 32)
                        if u == 0:
                            act.wait_ge(prep_t, 2)
                        k, h0 = (u // 2) % CHUNK, (u % 2) * HROWS
                        dst = XH[:, k, :, h0:h0 + HROWS, :]
                    else:
                        act.wait_ge(L["xt"], u + 1)
                        dst = xtile(u).bitcast(F16).rearrange("p s (h i e) -> p s h i e", i=32, e=2)[:, :, :, :, 0]
                    act.activation(dst, rows(DV[:, u % 2, :, :]), ACT.Copy).then_inc(L["hi"], 1)

            for t in range(TILES // 2 + 1):
                ln_step(0, t, TILES // 2)
            for t in range(TILES // 2, TILES + 1):
                ln_step(0, t, TILES, TILES // 2)
            def keep_tiles(t, dst, slot, done):
                a, lo, hi = xslab(t, dst)
                act.dma_start(a, STG[:, slot, 0:2, :]).then_inc(done, 16)
                act.dma_start(lo, STG[0:C1, slot, 2, :]).then_inc(done, 16)
                act.dma_start(hi, STG[C1:P, slot, 2, :]).then_inc(done, 16)

            for t in range(TILES + 3):
                if t <= TILES:
                    ln_step(1, t, TILES)
                if 1 <= t <= TILES:
                    act.wait_ge(ln[1]["xt"], t)
                    keep_tiles(t - 1, x1_d, (t - 1) % 2, st_x1[(t - 1) % 2])
                if 0 <= t - 3:
                    act.wait_ge(ln[1]["tt"], t - 2)
                    keep_tiles(t - 3, tn_d, 2 + (t - 3) % 2, st_tn[(t - 3) % 2])
            for s in range(FT + LAGF):
                if s < FT:
                    for m in range(MT):
                        c = s * MT + m
                        act.wait_ge(mm1, c + 1)
                        if m == 0 and s >= YR:
                            act.wait_ge(mm2[1], s - YR + 1)
                        if m == 0 and s == 8:
                            for e in range(2):
                                act.wait_ge(st_x1[e], 48 * PAIRS)
                                act.wait_ge(st_tn[e], 48 * PAIRS)
                        act.activation(Y[:, s % YR, m, :], m1p[c % 4][:, :], ACT.Identity, bias=b1s[:, m:m + 1],
                                       scale=1.0).then_inc(ev1, 1)
                u = s - LAGA
                if 0 <= u < FT:
                    act.wait_ge(gsc, u // GT + 1)
                    act.activation(Y[:, u % YR, :, :], Y[:, u % YR, :, :], ACT.Gelu, scale=gm[:, 3:4]) \
                        .then_inc(gelu, 1)
                    act.wait_ge(hs, u + 1)
                    if u >= 2:
                        act.wait_ge(mm2[1], u - 1)
                    act.activation(HI[:, u % 2, :, :], Y[:, u % YR, :, :], ACT.Copy).then_inc(hi2, 1)

        @block.vector
        def _(dve):
            v = nc.vector
            rp1, rp2 = HID // GROUPS // 3, C // GROUPS
            dve.wait_ge(ld_k, 32)
            v.memset(kraw[C1:P, 1, :, :], 0.0).then_inc(ker_step, 1)
            v.memset(kpad, 0.0).then_inc(ker_step, 1)
            dve.wait_ge(ker_step, 2)
            fwd, rev = slice(None), slice(None, None, -1)
            n = 2

            def rot(s, k):
                w = kraw[:, s, :, :]
                if k == 1:
                    return w[:, :, rev].rearrange("p a b -> p b a")
                if k == 2:
                    return w[:, rev, rev]
                return w[:, rev, :].rearrange("p a b -> p b a")
            for k in (1, 2, 3):
                for s in range(2):
                    v.tensor_tensor(out=kacc[:, s, :, :], in0=(kraw if k == 1 else kacc)[:, s, :, :],
                                    in1=rot(s, k), op=ALU.add).then_inc(ker_step, 1)
                n += 2
                dve.wait_ge(ker_step, n)
            v.tensor_scalar(kacc, kacc, 0.25 * WSC, None, ALU.mult).then_inc(bias_step, 1)
            dve.wait_ge(bias_step, 1)
            kr = kpad.rearrange("p s t (a e) -> p s t a e", e=2)
            t0 = QW - 1 - PAD
            for s in range(2):
                src = kacc[:, s, :, :].rearrange("p a b -> p b a")[:, rev, :]
                dsth = kr[:, s, t0:t0 + KS, :, 0]
                v.tensor_copy(dsth, src).then_inc(bias_step, 1)
            dve.wait_ge(bias_step, 3)
            for s in range(2):
                src = kacc[:, s, :, :].rearrange("p a b -> p b a")[:, rev, :]
                dsth = kr[:, s, t0:t0 + KS, :, 0]
                dstl = kr[:, s, t0:t0 + KS, :, 1]
                v.tensor_tensor(out=dstl, in0=src, in1=dsth, op=ALU.subtract).then_inc(bias_step, 1)
            dve.wait_ge(bias_step, 5)
            v.memset(wsum[:, :], 0.0).then_inc(ker_step, 1)
            dve.wait_ge(ker_step, 9)
            dve.wait_ge(ld_w, 160)
            v.reduce_sum(wsum[0:rp1, 0:GROUPS], w1f[0:rp1, :, :], axis=AX.X).then_inc(prep_sum, 1)
            v.reduce_sum(wsum[0:rp2, GROUPS:], w2f[0:rp2, :, :], axis=AX.X).then_inc(prep_sum, 1)
            dve.wait_ge(prep_tot, 1)
            v.tensor_scalar(wmean[:, 0:GROUPS], stp[:, 0:GROUPS], -1.0 / (3 * rp1 * C), None, ALU.mult) \
                .then_inc(bias_step, 1)
            v.tensor_scalar(wmean[:, GROUPS:], stp[:, GROUPS:2 * GROUPS], -1.0 / (rp2 * HID), None, ALU.mult) \
                .then_inc(bias_step, 1)
            dve.wait_ge(bias_step, 7)
            dve.wait_ge(ld_b, 48)
            v.tensor_scalar(b1s[:, :], b1s[:, :], XSC, None, ALU.mult).then_inc(bias_step, 1)
            v.tensor_scalar(b2s[:, 0:1], b2s[:, 0:1], HSC, None, ALU.mult).then_inc(bias_step, 1)
            v.tensor_scalar(b2s[0:C1, 1:2], b2s[0:C1, 1:2], HSC, None, ALU.mult).then_inc(bias_step, 1)
            v.memset(W1A[:, GROUPS * 3 * rp1:], 0.0).then_inc(bias_step, 1)
            v.memset(W1B[:, GROUPS * 3 * rp1:], 0.0).then_inc(bias_step, 1)
            v.memset(W2T[:, :, GROUPS * rp2:], 0.0).then_inc(bias_step, 1)
            dve.wait_ge(st_ker, 32)
            v.memset(view(46080, 3584), 0.0).then_inc(zeroed, 1)
            dve.wait_ge(bias_step, 13)
            v.memset(am2[:, :], 0.0).then_inc(prep_mean, 1)
            dve.wait_ge(prep_t, 1)
            for dst, src in ((W1A, t1a), (W1B, t1b)):
                for g in range(GROUPS):
                    o = dst[:, g * 3 * rp1:(g + 1) * 3 * rp1].rearrange("p (q r) -> p r q", r=3)
                    i = src[:, g * 3 * 64:(g + 1) * 3 * 64].rearrange("p (r q) -> p r q", r=3)[:, :, 0:rp1]
                    v.tensor_copy(o, i).then_inc(prep_done, 1)
            dve.wait_ge(prep_t, 2)
            for m in range(MT):
                v.tensor_copy(W2T[:, m, 0:GROUPS * rp2].rearrange("p (g q) -> p g q", g=GROUPS),
                              t2[m]).then_inc(prep_done, 1)

            def bring(t):
                dve.wait_ge(ld_x[t % 4], 48 * (t // 4 + 1))
                v.transpose(xtile(t), STG[:, t % 4, :, :]).then_inc(ln[0]["xb"], 1)
                dve.wait_ge(ln[0]["xb"], t + 1)

            def red1(p, t):
                v.reduce_sum(S1[:, t % 2, :].rearrange("p (s h) -> p s h", s=3), rows(xtile(t)), axis=AX.X) \
                    .then_inc(ln[p]["s1"], 1)

            def red2(p, t):
                dve.wait_ge(ln[p]["sq"], t + 1)
                v.reduce_sum(S2[:, t % 2, :], sqp[:, :].rearrange("p (a i) -> p a i", i=32), axis=AX.X) \
                    .then_inc(ln[p]["s2"], 1)

            def sub(p, t):
                dve.wait_ge(ln[p]["mu"], t + 1)
                if t >= 2:
                    dve.wait_ge(ln[p]["lo"], t - 1)
                elif p == 1:
                    dve.wait_ge(ln[0]["lo"], TILES)
                v.tensor_tensor(out=rows(DV[:, t % 2, :, :]), in0=rows(xtile(t)), in1=per_row(MU, t % 2),
                                op=ALU.subtract).then_inc(ln[p]["d"], 1)

            def recip(p, t):
                dve.wait_ge(ln[p]["sd"], t + 1)
                v.reciprocal(RS[:, t % 2, :], SD[:, t % 2, :]).then_inc(ln[p]["r"], 1)

            def low(p, t):
                dve.wait_ge(ln[p]["hi"], t + 1)
                d = rows(DV[:, t % 2, :, :])
                if p == 0:
                    k, h0 = (t // 2) % CHUNK, (t % 2) * HROWS
                    v.tensor_tensor(out=XL[:, k, :, h0:h0 + HROWS, :], in0=d, in1=XH[:, k, :, h0:h0 + HROWS, :],
                                    op=ALU.subtract).then_inc(ln[p]["lo"], 1)
                else:
                    w = xtile(t).bitcast(F16).rearrange("p s (h i e) -> p s h i e", i=32, e=2)
                    v.tensor_tensor(out=w[:, :, :, :, 1], in0=d, in1=w[:, :, :, :, 0],
                                    op=ALU.subtract).then_inc(ln[p]["lo"], 1)
                    dve.wait_ge(ln[p]["lo"], t + 1)
                    if t >= 2:
                        dve.wait_ge(st_tn[t % 2], 48 * (t // 2))
                    v.transpose(STG[:, 2 + t % 2, :, :], xtile(t)).then_inc(ln[p]["tt"], 1)

            def keep(t):
                if t >= 2:
                    dve.wait_ge(st_x1[t % 2], 48 * (t // 2))
                v.transpose(STG[:, t % 2, :, :], xtile(t)).then_inc(ln[1]["xt"], 1)

            def add_conv(g, i, r, chunk, done):
                dve.wait_ge(conv[g], done)
                ns = 2 if g == 0 else 1
                xs = XB[:, chunk * CHUNK:(chunk + 1) * CHUNK, (0 if g == 0 else 2):(2 if g == 0 else 3), :]
                xs = xs.rearrange("p k s (h i) -> p k s h i", i=32)
                xs = xs[:, :, :, :, bass.ds(i, 1)] if not isinstance(i, int) else xs[:, :, :, :, i:i + 1]
                xs = xs.rearrange("p k s h o -> p k (s h o)")
                v.scalar_tensor_tensor(out=xs, in0=cps[g][r][:, 0:CHUNK * ns * H].rearrange("p (k n) -> p k n", k=CHUNK),
                                       scalar=1.0 / (XSC * WSC), in1=xs, op0=ALU.mult, op1=ALU.add) \
                    .then_inc(cadd[g], 1)

            def ln0(t, t1):
                t0 = t1 - TILES // 2
                if t < t1:
                    bring(t)
                    red1(0, t)
                if t0 <= t - 2:
                    low(0, t - 2)
                if t0 <= t - 1 < t1:
                    red2(0, t - 1)
                if t < t1:
                    sub(0, t)
                if t0 <= t - 1 < t1:
                    recip(0, t - 1)

            for t in range(0, 10):
                ln0(t, 8)
            with dve.Fori(0, 16) as m:
                for r in range(2):
                    for g in range(2):
                        add_conv(g, 2 * m + r, r, 0, 2 * m + r + 1)
            for t in range(8, 18):
                ln0(t, 16)

            def ln1_a(t):
                if t < TILES:
                    red1(1, t)
                    keep(t)

            def ln1_b(t):
                if 0 <= t - 2:
                    low(1, t - 2)
                if 0 <= t - 1 < TILES:
                    red2(1, t - 1)

            def ln1_c(t):
                if t < TILES:
                    sub(1, t)

            def ln1_d(t):
                if 0 <= t - 1 < TILES:
                    recip(1, t - 1)

            dve.wait_ge(cadd[0], 32)
            dve.wait_ge(cadd[1], 32)
            for m in range(8):
                for n4, part in enumerate((ln1_a, ln1_b, ln1_c, ln1_d)):
                    i = 4 * m + n4
                    for g in range(2):
                        add_conv(g, i, i % 2, 1, 32 + i + 1)
                    part(m)
            dve.wait_ge(cadd[0], 64)
            dve.wait_ge(cadd[1], 64)
            for t in range(8, 18):
                ln1_a(t); ln1_b(t); ln1_c(t); ln1_d(t)

            for s in range(FT + LAGF):
                if 1 <= s <= FT:
                    u = s - 1
                    dve.wait_ge(ev1, MT * (u + 1))
                    v.tensor_reduce(am[:, u % GT:u % GT + 1], Y[:, u % YR, :, :], AX.XY, ALU.max,
                                    apply_absolute_value=True).then_inc(amx, 1)
                    if u % GT == GT - 1:
                        dve.wait_ge(amx, s)
                        v.tensor_reduce(gm[:, 0:1], am[:, 0:GT], AX.X, ALU.max).then_inc(gmx, 1)
                u = s - LAGA
                if 0 <= u < FT:
                    dve.wait_ge(gelu, u + 1)
                    v.tensor_scalar(Y[:, u % YR, :, :], Y[:, u % YR, :, :], HSC, HSC * CLIP, ALU.mult, ALU.min) \
                        .then_inc(hs, 1)
                u = s - LAGE
                if 0 <= u < FT:
                    for e in range(2):
                        n = P if e == 0 else C1
                        dve.wait_ge(mm2[e], u + 1)
                        if u >= Y2R:
                            dve.wait_ge(fin, 2 * (u - Y2R) + 1 + e)
                        v.tensor_scalar(Y2[0:n, u % Y2R, e, :], m2p[e][u % 2][0:n, :], b2s[0:n, e:e + 1], None,
                                        ALU.add).then_inc(ev2, 1)
                    dve.wait_ge(ev2, 2 * (u + 1))
                    for e in range(2):
                        n = P if e == 0 else C1
                        c = (u % GT) * 2 + e
                        v.tensor_reduce(am2[0:n, c:c + 1], Y2[0:n, u % Y2R, e, :], AX.X, ALU.max,
                                        apply_absolute_value=True).then_inc(amx2, 1)
                    if u % GT == GT - 1:
                        dve.wait_ge(amx2, 2 * (u + 1))
                        v.tensor_reduce(gm[:, 4:5], am2[:, :], AX.X, ALU.max).then_inc(gmx2, 1)
                if 0 < s <= FT and s % GT == 0:
                    g = s // GT
                    dve.wait_ge(gall, g)
                    v.tensor_scalar(gm[:, 2:3], gm[:, 1:2], 1.0 / XSC, QEPS, ALU.mult, ALU.add).then_inc(gsc_t, 1)
                    dve.wait_ge(gsc_t, 2 * g - 1)
                    v.reciprocal(gm[:, 2:3], gm[:, 2:3]).then_inc(gsc_t, 1)
                    dve.wait_ge(gsc_t, 2 * g)
                    if g >= 2:
                        dve.wait_ge(gelu, GT * (g - 1))
                    v.tensor_scalar(gm[:, 3:4], gm[:, 2:3], QB / XSC, None, ALU.mult).then_inc(gsc, 1)
                u = s - LAGF
                if 0 <= u < FT:
                    dve.wait_ge(gsc2, u // GT + 1)
                    for e in range(2):
                        n = P if e == 0 else C1
                        v.tensor_scalar(Y2[0:n, u % Y2R, e, :], Y2[0:n, u % Y2R, e, :], gm[0:n, 7:8], CLIP,
                                        ALU.mult, ALU.min).then_inc(clipd, 1)
                    dve.wait_ge(ld_xo[u % 2], 32 * (u // 2 + 1))
                    for e in range(2):
                        n = P if e == 0 else C1
                        dve.wait_ge(clipd, 2 * u + 1 + e)
                        v.scalar_tensor_tensor(out=XO[0:n, u % 2, e, :], in0=Y2[0:n, u % Y2R, e, :], scalar=-CLIP,
                                               in1=XO[0:n, u % 2, e, :], op0=ALU.max, op1=ALU.add).then_inc(fin, 1)
                u = s - LAGE
                if 0 < u <= FT and u % GT == 0:
                    g = u // GT
                    dve.wait_ge(gall2, g)
                    v.tensor_scalar(gm[:, 6:7], gm[:, 5:6], 1.0 / HSC, QEPS, ALU.mult, ALU.add).then_inc(gsc2_t, 1)
                    dve.wait_ge(gsc2_t, 2 * g - 1)
                    v.reciprocal(gm[:, 6:7], gm[:, 6:7]).then_inc(gsc2_t, 1)
                    dve.wait_ge(gsc2_t, 2 * g)
                    v.tensor_scalar(gm[:, 7:8], gm[:, 6:7], QB / HSC, None, ALU.mult).then_inc(gsc2, 1)

        @block.tensor
        def _(pe):
            t = nc.tensor
            rp1, rp2 = HID // GROUPS // 3, C // GROUPS
            pe.wait_ge(consts, 16)
            pe.wait_ge(prep_sum, 2)
            t.matmul(stp[:, 0:2 * GROUPS], ones[:, :], wsum[:, :], start=True, stop=True).then_inc(prep_tot, 1)
            pe.wait_ge(prep_sign, 2 * GROUPS)
            for g in range(GROUPS):
                for r in range(3):
                    c = (3 * g + r) * 64
                    t.transpose(t1a[:, c:c + rp1], w1s[0:rp1, g, r, 0:P], ident[0:rp1, 0:rp1])
                    t.transpose(t1b[:, c:c + rp1], w1s[0:rp1, g, r, C1:C], ident[0:rp1, 0:rp1])
                    last = t.transpose(t1b[0:C1, c:c + rp1], w1s[0:rp1, g, r, P:C], ident[0:rp1, 0:rp1])
            last.then_inc(prep_t, 1)
            for m in range(MT):
                for g in range(GROUPS):
                    last = t.transpose(t2[m][:, g, :], w2s[0:rp2, g, m, :], ident[0:rp2, 0:rp2])
            last.then_inc(prep_t, 1)
            pe.wait_ge(prep_done, 2 * GROUPS + MT)

            def channel_sums(out0, s):
                for img, edge in ((0, sumlo), (1, sumhi)):
                    o = stp[:, out0 + img * HROWS:out0 + (img + 1) * HROWS]
                    t.matmul(o, sumall[:, :], s[:, img * HROWS:(img + 1) * HROWS], start=True, stop=False)
                    last = t.matmul(o, edge[:, :], s[:, 2 * HROWS:NST], start=False, stop=True)
                return last

            def sums1(p, u):
                pe.wait_ge(ln[p]["s1"], u + 1)
                if u >= 2:
                    pe.wait_ge(ln[p]["sd"], u - 1)
                elif p == 1 and u == 0:
                    pe.wait_ge(ln[0]["sd"], TILES)
                channel_sums((u % 2) * 32, S1[:, u % 2, :]).then_inc(ln[p]["mps"], 1)

            def sums2(p, u, last):
                pe.wait_ge(ln[p]["s2"], u + 1)
                pe.wait_ge(ln[p]["mu"], min(u + 2, last))
                channel_sums(64 + (u % 2) * 32, S2[:, u % 2, :]).then_inc(ln[p]["vps"], 1)

            def conv_channel(i, r, band_fill, before):
                for g in range(2):
                    pe.wait_ge(ld_band[g][r], band_fill)
                    if before is not None:
                        pe.wait_ge(cadd[g], before)
                    ns = 2 if g == 0 else 1
                    ps = cps[g][r][:, 0:CHUNK * ns * H].rearrange("p (k s h) -> p k s h", k=CHUNK, s=ns)
                    order = [PAD] + [a for a in range(KS) if a != PAD]
                    for kh in order:
                        lo, hi, sl = tap(g, kh - PAD)
                        for part, src in ((0, XH), (0, XL), (1, XH)):
                            mv = src[:, :, sl, lo + kh - PAD:hi + kh - PAD, :]
                            mv = mv[:, :, :, :, bass.ds(i, 1)] if not isinstance(i, int) else mv[:, :, :, :, i:i + 1]
                            mv = mv.rearrange("p k s h o -> p k s (h o)")
                            last = t.matmul(ps[:, :, :, lo:hi], BD[:, g, r, :, 2 * kh + part], mv,
                                            start=(kh == PAD and part == 0 and src is XH),
                                            stop=(kh == order[-1] and part == 1))
                    last.then_inc(conv[g], 1)

            def ln0(t_, t0, t1):
                if t_ < t1:
                    sums1(0, t_)
                if t0 <= t_ - 1:
                    sums2(0, t_ - 1, t1)

            for u in range(9):
                ln0(u, 0, 8)
            pe.wait_ge(ln[0]["lo"], 8)
            conv_channel(0, 0, 64, None)
            conv_channel(1, 1, 64, None)
            with pe.Fori(1, 16) as m:
                for r in range(2):
                    conv_channel(2 * m + r, r, 64 * m + 64, 2 * m + r - 1)
            for u in range(8, 17):
                ln0(u, 8, 16)
            pe.wait_ge(ln[0]["lo"], 16)
            def conv2(i, r, m2):
                conv_channel(i, r, 64 * (16 + m2) + 64, 32 + 2 * m2 + r - 1)

            def second(kk):
                for e in range(2):
                    conv2(8 * kk + 4 * e, 0, 4 * kk + 2 * e)
                    conv2(8 * kk + 4 * e + 1, 1, 4 * kk + 2 * e)
                    yield e
                    conv2(8 * kk + 4 * e + 2, 0, 4 * kk + 2 * e + 1)
                    yield 2 + e
                    conv2(8 * kk + 4 * e + 3, 1, 4 * kk + 2 * e + 1)

            def stat_step(kk, e, first):
                base = 2 * kk
                if e < 2:
                    pe.wait_ge(ln[1]["s1"], base + e + 1)
                    if first:
                        if e == 0:
                            pe.wait_ge(ln[0]["sd"], TILES)
                    else:
                        pe.wait_ge(ln[1]["sd"], base + e - 1)
                    channel_sums(e * 32, S1[:, e, :]).then_inc(ln[1]["mps"], 1)
                else:
                    par = (e - 3) % 2
                    pe.wait_ge(ln[1]["s2"], base + e - 2)
                    pe.wait_ge(ln[1]["mu"], base + e - 1)
                    channel_sums(64 + par * 32, S2[:, par, :]).then_inc(ln[1]["vps"], 1)

            for e in second(0):
                if e != 2:
                    stat_step(0, e, True)
            with pe.Fori(1, 4) as kk:
                for e in second(kk):
                    stat_step(kk, e, False)
            for u in range(8, 17):
                if u < 16:
                    sums1(1, u)
                sums2(1, u - 1, TILES)

            pe.wait_ge(ln[1]["sd"], TILES)
            for s in range(FT + LAG2):
                if s < FT:
                    pe.wait_ge(ld_ta[s % 2], 48 * (s // 2 + 1))
                    ta = TA[:, s % 2, :].rearrange("p (n e) -> p n e", e=2)
                    tb = TB[:, s % 2, 1:1 + 2 * HALF].rearrange("p (n e) -> p n e", e=2)
                    for m in range(MT):
                        c = s * MT + m
                        if c >= 4:
                            pe.wait_ge(ev1, c - 3)
                        o = m1p[c % 4][:, :]
                        fs = slice(m * P, (m + 1) * P)
                        t.matmul(o, W1A[:, fs], ta[:, :, 0], start=True, stop=False)
                        t.matmul(o, W1A[:, fs], ta[:, :, 1], start=False, stop=False)
                        t.matmul(o, W1B[:, fs], tb[:, :, 0], start=False, stop=True).then_inc(mm1, 1)
                u = s - LAG2
                if 0 <= u < FT:
                    pe.wait_ge(lo2, u + 1)
                    lov = Y[:, u % YR, :, :].bitcast(F16).rearrange("p m (n e) -> p m n e", e=2)
                    for e in range(2):
                        n = P if e == 0 else C1
                        if u >= 2:
                            pe.wait_ge(ev2, 2 * (u - 2) + 1 + e)
                        for m in range(MT):
                            wt = W2T[:, m, 0:P] if e == 0 else W2T[:, m, P:C]
                            t.matmul(m2p[e][u % 2][0:n, :], wt, HI[:, u % 2, m, :], start=(m == 0), stop=False)
                            last = t.matmul(m2p[e][u % 2][0:n, :], wt, lov[:, m, :, 0], start=False,
                                            stop=(m == MT - 1))
                        last.then_inc(mm2[e], 1)


def kernel(x, L0_conv_weight, L0_ffn_W1, L0_ffn_b1, L0_ffn_W2, L0_ffn_b2):
    import numpy as np
    import concourse.bacc as bacc
    from concourse.bass_utils import run_bass_kernel_spmd

    nc = bacc.Bacc("TRN2", target_bir_lowering=False, num_devices=1)
    arrays, args = {}, []
    for name, a in (("x", np.asarray(x).reshape(B, C, PIX)), ("cw", L0_conv_weight), ("w1", L0_ffn_W1),
                    ("b1", L0_ffn_b1), ("w2", L0_ffn_W2), ("b2", L0_ffn_b2)):
        a = np.ascontiguousarray(a)
        arrays[name] = a
        args.append(nc.dram_tensor(name, a.shape, mybir.dt.from_np(a.dtype), kind="ExternalInput").ap())
    out = nc.dram_tensor("out", (B, C, PIX), F32, kind="ExternalOutput").ap()
    build(nc, *args, out)
    r = run_bass_kernel_spmd(nc, [arrays], core_ids=[0])
    return r.results[0]["out"].reshape(B, C, H, W)
```

```python
import concourse.bass as bass
from concourse import mybir
from contextlib import ExitStack

F32 = mybir.dt.float32
F16 = mybir.dt.float16
ALU = mybir.AluOpType
ACT = mybir.ActivationFunctionType
AX = mybir.AxisListType
RMAX = bass.bass_isa.ReduceOp.max

P = 128
B, C, H, W = 16, 192, 32, 32
PIX = H * W
HID = 4 * C
KS, PAD = 7, 3
GROUPS = 5
C1 = C - P
PAIRS = B // 2
CHUNK = PAIRS // 2
QW = 32
HALF = PIX // 2
QTR = HALF // 2
HROWS = H // 2
TILES = B
TC = TILES // 2
TW = 3 * HALF
NST = 3 * HROWS
PW = 3 * PIX
XSC, WSC = 16.0, 256.0
QB, QEPS = 128.0, 1e-5
CLIP = 127.99999237060547
HSC = 256.0
MT = HID // P
MH = MT // 2
RP1 = HID // GROUPS // 3
RP2 = C // GROUPS
FT = (B // GROUPS * GROUPS) * 2
GT = FT // GROUPS
OW = HALF + QTR
YR, Y2R = 8, 8
LAGA = GT
LAG2 = LAGA + 1
LAGE = LAG2 + 1
LAGF = LAGE + GT
LEAD = 2
RW = 64
KP = 2 * KS


def build(nc, x, cw, w1, b1, w2, b2, out):
    ctx = ExitStack()
    with ctx:
        arena = ctx.enter_context(nc.sbuf_tensor("arena", [P, 51712], F32))

        def view(at, words, dt=F32):
            v = arena[:, at:at + words]
            return v if dt == F32 else v.bitcast(dt)

        def sb(name, shape, dt=F32):
            return ctx.enter_context(nc.sbuf_tensor(name, shape, dt))

        def sem(name):
            return ctx.enter_context(nc.semaphore(name))

        ker_d = nc.dram_tensor("ker_d", (C, RW, KP), F16).ap()
        band_d = nc.dram_tensor("band_d", (C, QW, QW * KP), F16).ap()
        wt_d = nc.dram_tensor("wt_d", (P, 2 * HID + MT * C), F16).ap()
        x1_d = nc.dram_tensor("x1_d", (B, C, PIX), F32).ap()
        tn_d = nc.dram_tensor("tn_d", (B, C, PIX), F32).ap()

        A0, A1 = 0, CHUNK * PW
        A2 = A1 + CHUNK * PW
        A3 = A2 + 2 * 2 * 2 * QW * 4 * KP // 2
        A4 = A3 + CHUNK * PW
        A5 = A4 + 3 * TW
        assert A5 + 2 * TW == 51712

        def split_pair(at):
            return [view(at + e * CHUNK * PW // 2, CHUNK * PW // 2, F16)
                    .rearrange("p (k s h i) -> p k s h i", k=CHUNK, s=3, h=H) for e in range(2)]

        XC = [view(a, CHUNK * PW).rearrange("p (k s n) -> p k s n", k=CHUNK, s=3) for a in (A0, A3)]
        XN = [split_pair(A3), split_pair(A1)]
        BD = view(A2, A3 - A2, F16).rearrange("p (g r j c k) -> p g r j c k", g=2, r=2, j=2, c=P)
        STG = view(A4, 3 * TW).rearrange("p (r s n) -> p r s n", r=3, s=3)
        DV = view(A5, 2 * TW).rearrange("p (r s n) -> p r s n", r=2, s=3)
        w1f = view(A1, GROUPS * 3 * C).rearrange("p (g n) -> p g n", g=GROUPS)
        at = A1 + GROUPS * 3 * C
        w1s = view(at, GROUPS * 3 * C // 2, F16).rearrange("p (g r c) -> p g r c", g=GROUPS, r=3)
        at += GROUPS * 3 * C // 2
        w2f = view(at, GROUPS * HID).rearrange("p (g n) -> p g n", g=GROUPS)
        at += GROUPS * HID
        w2s = view(at, GROUPS * HID // 2, F16).rearrange("p (g m f) -> p g m f", g=GROUPS, m=MT)
        at += GROUPS * HID // 2
        kraw = view(at, 98).rearrange("p (s a b) -> p s a b", s=2, a=KS)
        kacc = view(at + 98, 98).rearrange("p (s a b) -> p s a b", s=2, a=KS)
        kpad = view(at + 196, 896, F16).rearrange("p (s t k) -> p s t k", s=2, t=RW)
        ones = view(at + 1092, P)
        assert at + 1220 <= A2
        WTN = 2 * HID + MT * C
        at = A2

        def weights(v):
            return (v[:, 0:HID], v[:, HID:2 * HID], v[:, 2 * HID:WTN].rearrange("p (m c) -> p m c", m=MT))
        wtb = view(A1, WTN // 2, F16)
        W1P, W1Q, W2P = weights(wtb)
        TAW = view(at, 2 * HALF).rearrange("p (r n) -> p r n", r=2)
        TA = view(at, 2 * HALF, F16).rearrange("p (r n) -> p r n", r=2)
        at += 2 * HALF
        TB = view(at, 2 * (HALF + 1), F16).rearrange("p (r n) -> p r n", r=2)
        at += 2 * (HALF + 1) + 2
        HI = view(at, MT * HALF, F16).rearrange("p (r m n) -> p r m n", r=2, m=MT)
        at += MT * HALF
        WT = view(at, WTN // 2, F16)
        W1A, W1B, W2T = weights(WT)
        at += WTN // 2
        assert at <= A3
        Y = view(A0, YR * MT * HALF).rearrange("p (r m n) -> p r m n", r=YR, m=MT)
        assert YR * MT * HALF <= A2
        Y2 = view(A3, Y2R * OW).rearrange("p (r n) -> p r n", r=Y2R)
        XO = view(A3 + Y2R * OW, 2 * OW).rearrange("p (r n) -> p r n", r=2)
        assert (Y2R + 2) * OW <= CHUNK * PW

        sumlo = sb("sumlo", [P, P])
        sumhi = sb("sumhi", [P, P])
        sumall = sb("sumall", [P, P])
        ident = sb("ident", [P, P], F16)
        b1s = sb("b1s", [P, MT])
        b2s = sb("b2s", [P, 2])
        eps = sb("eps", [P, 2])
        S1 = sb("S1", [P, 2, NST])
        S2 = sb("S2", [P, 2, NST])
        MU = sb("MU", [P, 2, NST])
        SD = sb("SD", [P, 2, NST])
        RS = sb("RS", [P, 2, NST])
        wsum = sb("wsum", [P, 2 * GROUPS])
        wmean = sb("wmean", [P, 2 * GROUPS])
        am = sb("am", [P, GT])
        am2 = sb("am2", [P, GT])
        gm = sb("gm", [P, 8])

        bank = [ctx.enter_context(nc.psum_tensor(f"bank{i}", [P, 512], F32)) for i in range(5)]
        sqp = ctx.enter_context(nc.psum_tensor("sqp", [P, TW], F32))
        cps = [[bank[0], bank[1]], [bank[2], bank[3]]]
        stp = bank[4]
        m1p = bank[0:4]
        m2p = [[bank[4][:, :], sqp[:, 0:512]], [sqp[:, 512:1024], sqp[:, 1024:1536]]]
        t1a = bank[0][:, 0:480].bitcast(F16)
        t1b = bank[1][:, 0:480].bitcast(F16)
        t2 = [bank[2 + m // 3][:, (m % 3) * 96:(m % 3) * 96 + 95].bitcast(F16).rearrange("p (g q) -> p g q", g=GROUPS)
              for m in range(MT)]

        ld_w = sem("ld_w"); ld_k = sem("ld_k"); ld_b = sem("ld_b")
        ld_x = [sem(f"ld_x{i}") for i in range(3)]
        ld_band = [[sem(f"ld_band{g}{r}") for r in range(2)] for g in range(2)]
        st_ker = sem("st_ker"); st_band = sem("st_band"); st_wt = sem("st_wt"); ld_wt = sem("ld_wt")
        st_x1 = sem("st_x1"); st_tn = sem("st_tn")
        consts = sem("consts"); zeroed = sem("zeroed")
        ker_step = sem("ker_step"); bias_step = sem("bias_step")
        prep_sum = sem("prep_sum"); prep_tot = sem("prep_tot"); prep_mean = sem("prep_mean")
        prep_sign = sem("prep_sign"); prep_t = sem("prep_t"); prep_done = sem("prep_done")
        names = "xb add s1 mps mu d sq s2 vps sd r xn hi lo xt tt"
        ln = [{n: sem(f"ln{p}_{n}") for n in names.split()} for p in range(2)]
        conv = [sem("conv0"), sem("conv1")]
        cadd = [sem("cadd0"), sem("cadd1")]
        cev = [sem("cev0"), sem("cev1")]
        ld_ta = [sem(f"ld_ta{i}") for i in range(2)]
        ld_xo = [sem(f"ld_xo{i}") for i in range(2)]
        st_o = [sem(f"st_o{i}") for i in range(2)]
        st_tail = sem("st_tail")
        mm1 = sem("mm1"); ev1 = sem("ev1"); mm2 = [sem("mm2a"), sem("mm2b")]; ev2 = sem("ev2")
        amx = sem("amx"); amx2 = sem("amx2")
        gmx = sem("gmx"); gall = sem("gall"); gsc_t = sem("gsc_t"); gsc = sem("gsc")
        gmx2 = sem("gmx2"); gall2 = sem("gall2"); gsc2_t = sem("gsc2_t"); gsc2 = sem("gsc2")
        gelu = sem("gelu"); hs = sem("hs"); hi2 = sem("hi2"); lo2 = sem("lo2")
        clipd = sem("clipd"); fin = sem("fin")

        block = ctx.enter_context(nc.Block())

        def xslab(t, dram):
            k, cols = t // 2, slice((t % 2) * HALF, (t % 2 + 1) * HALF)
            return (dram[2 * k:2 * k + 2, 0:P, cols].rearrange("b c n -> c b n"),
                    dram[2 * k, P:C, cols], dram[2 * k + 1, P:C, cols])

        def load_x(eng, t, slot):
            a, lo, hi = xslab(t, x)
            eng.dma_start(STG[:, slot, 0:2, :], a).then_inc(ld_x[slot], 16)
            eng.dma_start(STG[0:C1, slot, 2, :], lo).then_inc(ld_x[slot], 16)
            eng.dma_start(STG[C1:P, slot, 2, :], hi).then_inc(ld_x[slot], 16)

        def xtile(t):
            return XC[t // TC][:, (t // 2) % CHUNK, :, (t % 2) * HALF:(t % 2 + 1) * HALF]

        def source(p, t):
            return DV[:, t % 2, :, :] if p == 0 and t >= TC else xtile(t)

        def part(p, t, e):
            if p == 0:
                k, h0 = (t // 2) % CHUNK, (t % 2) * HROWS
                return XN[t // TC][e][:, k, :, h0:h0 + HROWS, :]
            return xtile(t).bitcast(F16).rearrange("p s (h i e) -> p s h i e", i=QW, e=2)[:, :, :, :, e]

        def rows(v):
            return v.rearrange("p s (h i) -> p s h i", i=QW)

        def per_row(v, par):
            return v[:, par, :].rearrange("p (s h) -> p s h", s=3).unsqueeze(3).to_broadcast([P, 3, HROWS, QW])

        def channel(v, i):
            return v[:, :, :, :, i:i + 1] if isinstance(i, int) else v[:, :, :, :, bass.ds(i, 1)]

        def conv_words(g, chunk, i):
            ns = 2 - g
            v = XC[chunk][:, :, 2 * g:2 * g + ns, :].rearrange("p k s (h i) -> p k s h i", i=QW)
            return channel(v, i).rearrange("p k s h o -> p k (s h o)"), \
                cps[g][i % 2 if isinstance(i, int) else 0][:, 0:CHUNK * ns * H].rearrange("p (k n) -> p k n", k=CHUNK)

        def low_half(u):
            return Y[:, u % YR, :, :].bitcast(F16).rearrange("p m (n e) -> p m n e", e=2)[:, :, :, 0]

        def halves(dram, b, cols):
            return [dram[b, P:C, cols.start + e * QTR:cols.start + (e + 1) * QTR] for e in range(2)]

        @block.sync
        def _(sp):
            sp.dma_start(kraw[:, 0, :, :], cw[0:P, 0, :, :]).then_inc(ld_k, 16)
            sp.dma_start(kraw[0:C1, 1, :, :], cw[P:C, 0, :, :]).then_inc(ld_k, 16)
            for t in range(3):
                load_x(sp, t, t)
            sp.wait_ge(ker_step, 13)
            sp.dma_start(ker_d[0:P, :, :], kpad[:, 0, :, :]).then_inc(st_ker, 16)
            sp.dma_start(ker_d[P:C, :, :], kpad[0:C1, 1, :, :]).then_inc(st_ker, 16)
            for g in range(GROUPS):
                sp.dma_start(w1f[0:RP1, g, :], w1[g * 3 * RP1:(g + 1) * 3 * RP1, :]
                             .rearrange("(p r) c -> p (r c)", r=3)).then_inc(ld_w, 16)
                sp.dma_start(w2f[0:RP2, g, :], w2[g * RP2:(g + 1) * RP2, :]).then_inc(ld_w, 16)
            sp.wait_ge(st_ker, 32)
            for n in range(4):
                c0, cn = n * (C // 4), C // 4
                src = bass.AP(ker_d.tensor, c0 * RW * KP + (QW - 1) * KP, [[RW * KP, cn], [-KP, QW], [1, QW * KP]])
                sp.dma_start(band_d[c0:c0 + cn, :, :], src).then_inc(st_band, 16)
            sp.dma_start(b1s[:, :], b1.rearrange("(m p) -> p m", p=P), allow_slow_non_contiguous=True).then_inc(ld_b, 16)
            sp.dma_start(b2s[:, 0:1], b2[0:P].rearrange("(p o) -> p o", o=1)).then_inc(ld_b, 16)
            for e in range(2):
                sp.dma_start(b2s[e * C1:(e + 1) * C1, 1:2], b2[P:C].rearrange("(p o) -> p o", o=1)).then_inc(ld_b, 16)

            def next_x(t):
                sp.wait_ge(ln[0]["xb"], t - 2)
                load_x(sp, t, t % 3)

            for t in range(3, TC - 1):
                next_x(t)
            sp.wait_ge(st_band, 64)
            sp.wait_ge(zeroed, 1)

            def load_band(pair, r, done):
                for g in range(2):
                    if done is not None:
                        sp.wait_ge(conv[g], done)
                    for q in range(4):
                        c = (q if g == 0 else 4 + q % 2) * QW + 2 * pair
                        src = band_d[bass.ds(c, 2), :, :].rearrange("j w n -> w j n")
                        dst = BD[q * QW:(q + 1) * QW, g, r, :, q * QW:(q + 1) * QW, :].rearrange("p j c k -> p j (c k)")
                        sp.dma_start(dst, src).then_inc(ld_band[g][r], 16)

            load_band(0, 0, None)
            load_band(1, 1, None)
            for t in range(TC - 1, TC + 3):
                next_x(t)
            for chunk in range(2):
                with sp.Fori(1 - chunk, 8) as m:
                    load_band(2 * m, 0, 4 * m - 2 + 32 * chunk)
                    load_band(2 * m + 1, 1, 4 * m + 32 * chunk)

            def load_tokens(s):
                b, half, cols = s // 2, s % 2, slice((s % 2) * HALF, (s % 2 + 1) * HALF)
                sp.wait_ge(st_tn, 48 * (b // 2 * 2 + half + 1))
                if s >= 2:
                    sp.wait_ge(mm1, MT * (s - 1))
                sp.dma_start(TAW[:, s % 2, :], tn_d[b, 0:P, cols]).then_inc(ld_ta[s % 2], 16)
                src = tn_d[b, P:C, cols].bitcast(F16)
                sp.dma_start(TB[0:C1, s % 2, 1:1 + 2 * HALF], src).then_inc(ld_ta[s % 2], 16)
                sp.dma_start(TB[C1:P, s % 2, 0:2 * HALF], src).then_inc(ld_ta[s % 2], 16)

            def load_x1(u):
                b, half, cols = u // 2, u % 2, slice((u % 2) * HALF, (u % 2 + 1) * HALF)
                sp.wait_ge(st_x1, 48 * (b // 2 * 2 + half + 1))
                if u >= 2:
                    sp.wait_ge(st_o[u % 2], 48 * (u // 2))
                sp.dma_start(XO[:, u % 2, 0:HALF], x1_d[b, 0:P, cols]).then_inc(ld_xo[u % 2], 16)
                for e, src in enumerate(halves(x1_d, b, cols)):
                    sp.dma_start(XO[e * C1:(e + 1) * C1, u % 2, HALF:OW], src).then_inc(ld_xo[u % 2], 16)

            def store(u):
                b, cols = u // 2, slice((u % 2) * HALF, (u % 2 + 1) * HALF)
                sp.wait_ge(fin, u + 1)
                sp.dma_start(out[b, 0:P, cols], XO[:, u % 2, 0:HALF]).then_inc(st_o[u % 2], 16)
                for e, dst in enumerate(halves(out, b, cols)):
                    sp.dma_start(dst, XO[e * C1:(e + 1) * C1, u % 2, HALF:OW]).then_inc(st_o[u % 2], 16)

            for g in range(2):
                sp.wait_ge(conv[g], 64)
            sp.wait_ge(st_wt, 16)
            sp.dma_start(WT, wt_d[:, :]).then_inc(ld_wt, 16)
            load_tokens(0)
            load_tokens(1)
            for s in range(FT + LAGF + 1):
                if s + 2 < FT:
                    load_tokens(s + 2)
                if 0 <= s - LAGF - 1 < FT:
                    store(s - LAGF - 1)
                if 0 <= s - LAGF + 1 < FT:
                    if s - LAGF + 1 == 0:
                        sp.wait_ge(ln[1]["tt"], TILES)
                    load_x1(s - LAGF + 1)
                if s == LAGF:
                    sp.wait_ge(st_x1, 48 * TILES)
                    sp.dma_start(out[B - 1, :, :], x1_d[B - 1, :, :]).then_inc(st_tail, 16)
            sp.wait_ge(st_tail, 16)
            for e in range(2):
                sp.wait_ge(st_o[e], 48 * (FT // 2))
            sp.wait_ge(st_tn, 48 * TILES)

        @block.gpsimd
        def _(pool):
            pool.memset(view(A2, A3 - A2), 0.0).then_inc(zeroed, 1)
            pool.memset(ident[:, :], 0.0).then_inc(consts, 1)
            pool.memset(sumlo[:, :], 0.0).then_inc(consts, 1)
            pool.memset(sumhi[:, :], 0.0).then_inc(consts, 1)
            pool.memset(sumall[:, :], 0.0).then_inc(consts, 1)
            pool.memset(ones, 1.0).then_inc(consts, 1)
            pool.memset(eps[:, 0:1], 1e-6 / (XSC * XSC)).then_inc(consts, 1)
            pool.memset(eps[:, 1:2], 1e-5 / (XSC * XSC)).then_inc(consts, 1)
            n = 7
            pool.wait_ge(consts, n)
            pool.affine_select(out=ident[:, :], in_=ident[:, :], compare_op=ALU.not_equal, fill=1.0, base=0,
                               pattern=[[-1, P]], channel_multiplier=1).then_inc(consts, 1)
            n += 1
            for q in range(4):
                for m in (sumall, sumlo if q < 2 else sumhi):
                    v = m[:, :].rearrange("p (a b) -> p a b", b=QW)
                    pool.affine_select(out=v, in_=v, compare_op=ALU.not_equal, fill=1.0, base=-q * QW,
                                       pattern=[[0, 4], [-1, QW]], channel_multiplier=1).then_inc(consts, 1)
                    n += 1
                    pool.wait_ge(consts, n)

            def ln_step(p, t, t0, t1):
                if t < t1:
                    pool.wait_ge(ln[p]["mu"], t + 1)
                    if t >= 2:
                        pool.wait_ge(ln[p]["lo"], t - 1)
                    elif p == 1:
                        pool.wait_ge(ln[0]["lo"], TILES)
                    pool.tensor_tensor(out=rows(DV[:, t % 2, :, :]), in0=rows(source(p, t)), in1=per_row(MU, t % 2),
                                       op=ALU.subtract).then_inc(ln[p]["d"], 1)
                u = t - 1
                if u >= t0:
                    pool.wait_ge(ln[p]["r"], u + 1)
                    v = rows(DV[:, u % 2, :, :])
                    pool.tensor_tensor(out=v, in0=v, in1=per_row(RS, u % 2), op=ALU.mult).then_inc(ln[p]["xn"], 1)

            for t in range(TC + 1):
                ln_step(0, t, 0, TC)
            for t in range(TC, TILES + 1):
                ln_step(0, t, TC, TILES)
            for t in range(TC + 1):
                ln_step(1, t, 0, TC)
            for s in range(-LEAD, FT + LAGF):
                t = s + LEAD + TC
                if t <= TILES:
                    ln_step(1, t, TC, TILES)
                if 1 <= s <= FT and s % GT == 0:
                    g = s // GT - 1
                    pool.wait_ge(gmx, g + 1)
                    pool.partition_all_reduce(gm[:, 1:2], gm[:, 0:1], P, RMAX).then_inc(gall, 1)
                u = s - LAGA
                if 0 <= u < FT:
                    for e in range(2):
                        ms = slice(e * MH, (e + 1) * MH)
                        pool.wait_ge(hi2, 2 * u + e + 1)
                        pool.tensor_tensor(out=low_half(u)[:, ms, :], in0=Y[:, u % YR, ms, :],
                                           in1=HI[:, u % 2, ms, :], op=ALU.subtract).then_inc(lo2, 1)
                u = s - LAGE
                if 0 <= u < FT and u % GT == GT - 1:
                    pool.wait_ge(gmx2, u // GT + 1)
                    pool.partition_all_reduce(gm[:, 5:6], gm[:, 4:5], P, RMAX).then_inc(gall2, 1)

        @block.scalar
        def _(act):
            def stat(dst, src, func, bias=None, **kw):
                def go(o, i, lo, hi):
                    b = {} if bias is None else {"bias": bias[lo:hi, :]}
                    return act.activation(o, i, func, **b, **kw)
                go(dst[:, 0:2 * HROWS], src[:, 0:2 * HROWS], 0, P)
                go(dst[0:C1, 2 * HROWS:NST], src[0:C1, 0:HROWS], 0, C1)
                return go(dst[C1:P, 2 * HROWS:NST], src[C1:P, HROWS:2 * HROWS], C1, P)

            def store_tile(t, dst, slot, done):
                a, lo, hi = xslab(t, dst)
                act.dma_start(a, STG[:, slot, 0:2, :]).then_inc(done, 16)
                act.dma_start(lo, STG[0:C1, slot, 2, :]).then_inc(done, 16)
                act.dma_start(hi, STG[C1:P, slot, 2, :]).then_inc(done, 16)

            def ln_parts(p, t, t0, t1):
                L = ln[p]
                u = t - 1
                if t < t1:
                    if p == 0 and TC < t < TILES - 2:
                        act.wait_ge(L["xb"], t)
                        load_x(act, t + 2, (t + 2) % 3)
                    act.wait_ge(L["mps"], t + 1)
                    stat(MU[:, t % 2, :], stp[:, (t % 2) * 32:(t % 2) * 32 + 32], ACT.Copy, scale=1.0 / C) \
                        .then_inc(L["mu"], 1)
                    if p == 1 and TC <= t < TILES - 1:
                        act.wait_ge(L["xb"], t - TC + 1)
                        load_x(act, t + 1, 2)
                yield
                if u >= t0:
                    act.wait_ge(L["vps"], u + 1)
                    stat(SD[:, u % 2, :], stp[:, 64 + (u % 2) * 32:96 + (u % 2) * 32], ACT.Sqrt,
                         bias=eps[:, p:p + 1], scale=1.0 / (C * XSC * XSC)).then_inc(L["sd"], 1)
                if t < t1:
                    act.wait_ge(L["d"], t + 1)
                    if t >= 1:
                        act.wait_ge(L["s2"], t)
                    act.activation(sqp[:, :].rearrange("p (s n) -> p s n", s=3), DV[:, t % 2, :, :], ACT.Square) \
                        .then_inc(L["sq"], 1)
                    if p == 1:
                        act.wait_ge(L["xt"], t + 1)
                        store_tile(t, x1_d, 0, st_x1)
                yield
                if u >= t0:
                    act.wait_ge(L["xn"], u + 1)
                    act.activation(part(p, u, 0), rows(DV[:, u % 2, :, :]), ACT.Copy).then_inc(L["hi"], 1)
                if p == 1 and t - 2 >= t0:
                    act.wait_ge(L["tt"], t - 1)
                    store_tile(t - 2, tn_d, 1, st_tn)
                yield

            def ln_step(p, t, t0, t1):
                for _ in ln_parts(p, t, t0, t1):
                    pass

            def signs(g):
                act.activation(w1s[0:RP1, g, :, :], w1f[0:RP1, g, :].rearrange("p (r c) -> p r c", r=3), ACT.Sign,
                               bias=wmean[0:RP1, g:g + 1], scale=1.0).then_inc(prep_sign, 1)
                act.activation(w2s[0:RP2, g, :, :], w2f[0:RP2, g, :].rearrange("p (m f) -> p m f", m=MT), ACT.Sign,
                               bias=wmean[0:RP2, GROUPS + g:GROUPS + g + 1], scale=1.0).then_inc(prep_sign, 1)

            for t in range(TC + 1):
                ln_step(0, t, 0, TC)
                if t == 3:
                    act.wait_ge(prep_mean, 2)
                if 3 <= t < 3 + GROUPS:
                    signs(t - 3)
            act.wait_ge(prep_done, 3 + 2 * GROUPS + MT)
            act.dma_start(wt_d[:, :], wtb).then_inc(st_wt, 16)
            for t in range(TC, TILES + 1):
                if t == TC + 1:
                    act.wait_ge(st_wt, 16)
                ln_step(0, t, TC, TILES)

            def evac(i):
                for g in range(2):
                    act.wait_ge(conv[g], QW + i + 1)
                    dst, src = conv_words(g, 1, i)
                    act.activation(dst, src, ACT.Copy, scale=1.0 / (XSC * WSC)).then_inc(cev[g], 1)

            for t in range(TC):
                evac(4 * t)
                evac(4 * t + 1)
                for n, _ in enumerate(ln_parts(1, t, 0, TC)):
                    if n < 2:
                        evac(4 * t + 2 + n)
            load_x(act, TC, 2)
            ln_step(1, TC, 0, TC)
            act.wait_ge(ln[1]["tt"], TC)
            store_tile(TC - 1, tn_d, 1, st_tn)

            for s in range(-LEAD, FT + LAGF):
                t = s + LEAD + TC
                if t <= TILES:
                    ln_step(1, t, TC, TILES)
                if t == TILES + 1:
                    act.wait_ge(ln[1]["tt"], TILES)
                    store_tile(TILES - 1, tn_d, 1, st_tn)
                if 0 <= s < FT:
                    for m in range(MT):
                        c = s * MT + m
                        act.wait_ge(mm1, c + 1)
                        if m == 0 and s >= YR:
                            act.wait_ge(mm2[1], s - YR + 1)
                        act.activation(Y[:, s % YR, m, :], m1p[c % 4][:, :], ACT.Identity, bias=b1s[:, m:m + 1],
                                       scale=1.0).then_inc(ev1, 1)
                u = s - LAGA
                if 0 <= u < FT:
                    act.wait_ge(gsc, u // GT + 1)
                    for e in range(2):
                        ms = slice(e * MH, (e + 1) * MH)
                        act.activation(Y[:, u % YR, ms, :], Y[:, u % YR, ms, :], ACT.Gelu, scale=gm[:, 3:4]) \
                            .then_inc(gelu, 1)
                    for e in range(2):
                        ms = slice(e * MH, (e + 1) * MH)
                        act.wait_ge(hs, 2 * u + e + 1)
                        if u >= 2:
                            act.wait_ge(mm2[1], u - 1)
                        act.activation(HI[:, u % 2, ms, :], Y[:, u % YR, ms, :], ACT.Copy).then_inc(hi2, 1)

        @block.vector
        def _(dve):
            v = nc.vector
            v.memset(kpad, 0.0).then_inc(ker_step, 1)
            dve.wait_ge(ld_k, 32)
            v.memset(kraw[C1:P, 1, :, :], 0.0).then_inc(ker_step, 1)
            dve.wait_ge(ker_step, 2)
            fwd, rev = slice(None), slice(None, None, -1)

            def rot(s, k):
                w = kraw[:, s, :, :]
                if k == 1:
                    return w[:, :, rev].rearrange("p a b -> p b a")
                if k == 2:
                    return w[:, rev, rev]
                return w[:, rev, :].rearrange("p a b -> p b a")
            n = 2
            for k in (1, 2, 3):
                for s in range(2):
                    v.tensor_tensor(out=kacc[:, s, :, :], in0=(kraw if k == 1 else kacc)[:, s, :, :], in1=rot(s, k),
                                    op=ALU.add).then_inc(ker_step, 1)
                n += 2
                dve.wait_ge(ker_step, n)
            v.tensor_scalar(kacc, kacc, 0.25 * WSC, None, ALU.mult).then_inc(ker_step, 1)
            dve.wait_ge(ker_step, 9)
            kr = kpad.rearrange("p s t (a e) -> p s t a e", e=2)
            t0 = QW - PAD - 1
            ends = [(kacc[:, s, :, :].rearrange("p a b -> p b a")[:, rev, :],
                     kr[:, s, t0:t0 + KS, :, 0], kr[:, s, t0:t0 + KS, :, 1]) for s in range(2)]
            for src, high, low in ends:
                v.tensor_copy(high, src).then_inc(ker_step, 1)
            dve.wait_ge(ker_step, 11)
            for src, high, low in ends:
                v.tensor_tensor(out=low, in0=src, in1=high, op=ALU.subtract).then_inc(ker_step, 1)

            def weight_sums():
                dve.wait_ge(ld_w, 160)
                v.memset(wsum[:, :], 0.0).then_inc(bias_step, 1)
                dve.wait_ge(bias_step, 1)
                v.reduce_sum(wsum[0:RP1, 0:GROUPS], w1f[0:RP1, :, :], axis=AX.X).then_inc(prep_sum, 1)
                v.reduce_sum(wsum[0:RP2, GROUPS:], w2f[0:RP2, :, :], axis=AX.X).then_inc(prep_sum, 1)

            def weight_means():
                dve.wait_ge(prep_tot, 1)
                v.tensor_scalar(wmean[:, 0:GROUPS], bank[0][:, 0:GROUPS], -1.0 / (3 * RP1 * C), None, ALU.mult) \
                    .then_inc(prep_mean, 1)
                v.tensor_scalar(wmean[:, GROUPS:], bank[0][:, GROUPS:2 * GROUPS], -1.0 / (RP2 * HID), None, ALU.mult) \
                    .then_inc(prep_mean, 1)
                dve.wait_ge(ld_b, 64)
                v.tensor_scalar(b1s[:, :], b1s[:, :], XSC, None, ALU.mult).then_inc(bias_step, 1)
                v.tensor_scalar(b2s[:, :], b2s[:, :], HSC, None, ALU.mult).then_inc(bias_step, 1)
                dve.wait_ge(bias_step, 3)

            def weight_copies():
                dve.wait_ge(prep_t, 1)
                v.memset(W1P[:, GROUPS * 3 * RP1:], 0.0).then_inc(prep_done, 1)
                v.memset(W1Q[:, GROUPS * 3 * RP1:], 0.0).then_inc(prep_done, 1)
                v.memset(W2P[:, :, GROUPS * RP2:], 0.0).then_inc(prep_done, 1)
                for dst, src in ((W1P, t1a), (W1Q, t1b)):
                    for g in range(GROUPS):
                        o = dst[:, g * 3 * RP1:(g + 1) * 3 * RP1].rearrange("p (q r) -> p r q", r=3)
                        i = src[:, g * 3 * 64:(g + 1) * 3 * 64].rearrange("p (r q) -> p r q", r=3)[:, :, 0:RP1]
                        v.tensor_copy(o, i).then_inc(prep_done, 1)
                dve.wait_ge(prep_t, 2)
                for m in range(MT):
                    v.tensor_copy(W2P[:, m, 0:GROUPS * RP2].rearrange("p (g q) -> p g q", g=GROUPS),
                                  t2[m]).then_inc(prep_done, 1)

            def low(p, t):
                dve.wait_ge(ln[p]["hi"], t + 1)
                v.tensor_tensor(out=part(p, t, 1), in0=rows(DV[:, t % 2, :, :]), in1=part(p, t, 0),
                                op=ALU.subtract).then_inc(ln[p]["lo"], 1)
                if p == 1:
                    dve.wait_ge(ln[p]["lo"], t + 1)
                    dve.wait_ge(st_tn, 48 * t) if t else None
                    v.transpose(STG[:, 1, :, :], xtile(t)).then_inc(ln[p]["tt"], 1)

            def bring(p, t):
                if p == 0:
                    dve.wait_ge(ld_x[t % 3], 48 * (t // 3 + 1))
                    if t >= TC:
                        dve.wait_ge(ln[0]["lo"], t - 1)
                    v.transpose(source(0, t), STG[:, t % 3, :, :]).then_inc(ln[0]["xb"], 1)
                    dve.wait_ge(ln[0]["xb"], t + 1)
                elif t >= TC:
                    n = t - TC + 1
                    dve.wait_ge(ld_x[2], 48 * (TILES // 3 + n))
                    dve.wait_ge(ln[1]["lo"], t - 1)
                    v.transpose(DV[:, t % 2, :, :], STG[:, 2, :, :]).then_inc(ln[1]["xb"], 1)
                    dve.wait_ge(ln[1]["xb"], n)
                    v.tensor_tensor(out=xtile(t), in0=xtile(t), in1=DV[:, t % 2, :, :], op=ALU.add) \
                        .then_inc(ln[1]["add"], 1)
                    dve.wait_ge(ln[1]["add"], n)

            def red1(p, t):
                v.reduce_sum(S1[:, t % 2, :].rearrange("p (s h) -> p s h", s=3), rows(source(p, t)), axis=AX.X) \
                    .then_inc(ln[p]["s1"], 1)
                if p == 1:
                    if t >= 1:
                        dve.wait_ge(st_x1, 48 * t)
                    v.transpose(STG[:, 0, :, :], xtile(t)).then_inc(ln[1]["xt"], 1)

            def red2(p, t):
                dve.wait_ge(ln[p]["sq"], t + 1)
                v.reduce_sum(S2[:, t % 2, :], sqp[:, :].rearrange("p (a i) -> p a i", i=QW), axis=AX.X) \
                    .then_inc(ln[p]["s2"], 1)

            def recip(p, t):
                dve.wait_ge(ln[p]["sd"], t + 1)
                v.reciprocal(RS[:, t % 2, :], SD[:, t % 2, :]).then_inc(ln[p]["r"], 1)

            def ln_parts(p, t, t0, t1):
                if t - 2 >= t0:
                    low(p, t - 2)
                yield
                if t < t1:
                    bring(p, t)
                    red1(p, t)
                yield
                if t0 <= t - 1 < t1:
                    red2(p, t - 1)
                yield
                if t0 <= t - 1 < t1:
                    recip(p, t - 1)
                yield

            def ln_step(p, t, t0, t1):
                for _ in ln_parts(p, t, t0, t1):
                    pass

            def add_conv(i):
                for g in range(2):
                    dve.wait_ge(conv[g], i + 1)
                    xs, ps = conv_words(g, 0, i)
                    v.scalar_tensor_tensor(out=xs, in0=ps, scalar=1.0 / (XSC * WSC), in1=xs, op0=ALU.mult,
                                           op1=ALU.add).then_inc(cadd[g], 1)

            for t in range(TC + 2):
                ln_step(0, t, 0, TC)
                if t == 1:
                    weight_sums()
                if t == 2:
                    weight_means()
            weight_copies()
            dve.wait_ge(prep_done, 3 + 2 * GROUPS + MT)
            for m in range(TC):
                for n, _ in enumerate(ln_parts(0, TC + m, TC, TILES)):
                    add_conv(4 * m + n)
            for t in (TILES, TILES + 1):
                ln_step(0, t, TC, TILES)
            for g in range(2):
                dve.wait_ge(cadd[g], QW)
            for t in range(TC + 2):
                ln_step(1, t, 0, TC)
            for g in range(2):
                dve.wait_ge(cev[g], QW)

            for s in range(-LEAD, FT + LAGF):
                t = s + LEAD + TC
                if t <= TILES + 1:
                    ln_step(1, t, TC, TILES)
                if 1 <= s <= FT:
                    u = s - 1
                    dve.wait_ge(ev1, MT * (u + 1))
                    v.tensor_reduce(am[:, u % GT:u % GT + 1], Y[:, u % YR, :, :], AX.XY, ALU.max,
                                    apply_absolute_value=True).then_inc(amx, 1)
                    if u % GT == GT - 1:
                        g = u // GT + 1
                        dve.wait_ge(amx, s)
                        v.tensor_reduce(gm[:, 0:1], am[:, :], AX.X, ALU.max).then_inc(gmx, 1)
                        dve.wait_ge(gall, g)
                        v.tensor_scalar(gm[:, 2:3], gm[:, 1:2], 1.0 / XSC, QEPS, ALU.mult, ALU.add).then_inc(gsc_t, 1)
                        dve.wait_ge(gsc_t, 2 * g - 1)
                        v.reciprocal(gm[:, 2:3], gm[:, 2:3]).then_inc(gsc_t, 1)
                        dve.wait_ge(gsc_t, 2 * g)
                        if g >= 2:
                            dve.wait_ge(gelu, 2 * GT * (g - 1))
                        v.tensor_scalar(gm[:, 3:4], gm[:, 2:3], QB / XSC, None, ALU.mult).then_inc(gsc, 1)
                u = s - LAGA
                if 0 <= u < FT:
                    for e in range(2):
                        ms = slice(e * MH, (e + 1) * MH)
                        dve.wait_ge(gelu, 2 * u + e + 1)
                        v.tensor_scalar(Y[:, u % YR, ms, :], Y[:, u % YR, ms, :], HSC, HSC * CLIP, ALU.mult, ALU.min) \
                            .then_inc(hs, 1)
                u = s - LAGF
                if 0 <= u < FT and u % GT == 0:
                    g = u // GT + 1
                    dve.wait_ge(gall2, g)
                    v.tensor_scalar(gm[:, 6:7], gm[:, 5:6], 1.0 / HSC, QEPS, ALU.mult, ALU.add) \
                        .then_inc(gsc2_t, 1)
                    dve.wait_ge(gsc2_t, 2 * g - 1)
                    v.reciprocal(gm[:, 6:7], gm[:, 6:7]).then_inc(gsc2_t, 1)
                    dve.wait_ge(gsc2_t, 2 * g)
                    v.tensor_scalar(gm[:, 7:8], gm[:, 6:7], QB / HSC, None, ALU.mult).then_inc(gsc2, 1)
                if 0 <= u < FT:
                    dve.wait_ge(gsc2, u // GT + 1)
                    v.tensor_scalar(Y2[:, u % Y2R, :], Y2[:, u % Y2R, :], gm[:, 7:8], CLIP, ALU.mult, ALU.min) \
                        .then_inc(clipd, 1)
                    dve.wait_ge(ld_xo[u % 2], 48 * (u // 2 + 1))
                    dve.wait_ge(clipd, u + 1)
                    v.scalar_tensor_tensor(out=XO[:, u % 2, :], in0=Y2[:, u % Y2R, :], scalar=-CLIP,
                                           in1=XO[:, u % 2, :], op0=ALU.max, op1=ALU.add).then_inc(fin, 1)
                u = s - LAGE
                if 0 <= u < FT:
                    if u == 0:
                        dve.wait_ge(ln[1]["tt"], TILES)
                    if u >= Y2R:
                        dve.wait_ge(fin, u - Y2R + 1)
                    for e, cols in ((0, slice(0, HALF)), (1, slice(HALF, OW))):
                        dve.wait_ge(mm2[e], u + 1)
                        v.tensor_scalar(Y2[:, u % Y2R, cols], m2p[e][u % 2][:, 0:cols.stop - cols.start],
                                        b2s[:, e:e + 1], None, ALU.add).then_inc(ev2, 1)
                    dve.wait_ge(ev2, 2 * (u + 1))
                    v.tensor_reduce(am2[:, u % GT:u % GT + 1], Y2[:, u % Y2R, :], AX.X, ALU.max,
                                    apply_absolute_value=True).then_inc(amx2, 1)
                    if u % GT == GT - 1:
                        dve.wait_ge(amx2, u + 1)
                        v.tensor_reduce(gm[:, 4:5], am2[:, :], AX.X, ALU.max).then_inc(gmx2, 1)

        @block.tensor
        def _(pe):
            t = nc.tensor

            def channel_sums(out0, s):
                for img, edge in ((0, sumlo), (1, sumhi)):
                    o = stp[:, out0 + img * HROWS:out0 + (img + 1) * HROWS]
                    t.matmul(o, sumall[:, :], s[:, img * HROWS:(img + 1) * HROWS], start=True, stop=False)
                    last = t.matmul(o, edge[:, :], s[:, 2 * HROWS:NST], start=False, stop=True)
                return last

            def sums1(p, u, par, after=None):
                pe.wait_ge(ln[p]["s1"], u + 1)
                if after == 0 and u == 0:
                    if p == 1:
                        pe.wait_ge(ln[0]["sd"], TILES)
                elif after == 1:
                    pe.wait_ge(ln[p]["mu"], u)
                else:
                    pe.wait_ge(ln[p]["sd"], u if after == 0 else u - 1)
                channel_sums(par * 32, S1[:, par, :]).then_inc(ln[p]["mps"], 1)

            def sums2(p, u, par, last=False):
                pe.wait_ge(ln[p]["s2"], u + 1)
                if last:
                    pe.wait_ge(ln[p]["sd"], u)
                else:
                    pe.wait_ge(ln[p]["mu"], u + 2)
                channel_sums(64 + par * 32, S2[:, par, :]).then_inc(ln[p]["vps"], 1)

            def conv_channel(chunk, i, j, r, fill, free, n):
                for g in range(2):
                    pe.wait_ge(ld_band[g][r], fill)
                    if free is not None:
                        pe.wait_ge(free[g], n)
                    ns = 2 - g
                    ps = cps[g][j][:, 0:CHUNK * ns * H].rearrange("p (k s h) -> p k s h", k=CHUNK, s=ns)
                    order = [PAD] + [a for a in range(KS) if a != PAD]
                    for kh in order:
                        dh = kh - PAD
                        lo, hi = max(0, -dh), min(H, H - dh)
                        for wpart, xpart in ((0, 0), (0, 1), (1, 0)):
                            mv = channel(XN[chunk][xpart][:, :, 2 * g:2 * g + ns, lo + dh:hi + dh, :], i)
                            last = t.matmul(ps[:, :, :, lo:hi], BD[:, g, r, j, :, 2 * kh + wpart],
                                            mv.rearrange("p k s h o -> p k s (h o)"),
                                            start=(kh == PAD and wpart == xpart == 0),
                                            stop=(kh == order[-1] and wpart == 1))
                    last.then_inc(conv[g], 1)

            def conv_phase(chunk, free, first_free, p, base):
                def eight(kk, first):
                    for n in range(8):
                        i = 8 * kk + n
                        if first and n < 2:
                            conv_channel(chunk, i, n % 2, (n // 2) % 2, 64 * (8 * chunk + 1), *first_free)
                        else:
                            conv_channel(chunk, i, n % 2, (n // 2) % 2,
                                         64 * (2 * kk + 1 + n // 4 + 8 * chunk), free, i - 1)
                        u = base + 2 * kk + n // 4
                        if n % 4 == 1:
                            sums1(p, u, (n // 4) % 2, n // 4 if first else None)
                        if n % 4 == 2 and not (first and n < 4):
                            sums2(p, u - 1, (n // 4 + 1) % 2)
                eight(0, True)
                with pe.Fori(1, 4) as kk:
                    eight(kk, False)
                sums2(p, base + TC - 1, 1, last=True)

            pe.wait_ge(consts, 16)
            for u in range(TC):
                sums1(0, u, u % 2, u)
                if u:
                    sums2(0, u - 1, (u - 1) % 2)
                if u == 1:
                    pe.wait_ge(prep_sum, 2)
                    t.matmul(bank[0][:, 0:2 * GROUPS], ones, wsum[:, :], start=True, stop=True).then_inc(prep_tot, 1)
            sums2(0, TC - 1, 1, last=True)
            pe.wait_ge(prep_sign, 2 * GROUPS)
            for g in range(GROUPS):
                for r in range(3):
                    c = (3 * g + r) * 64
                    t.transpose(t1a[:, c:c + RP1], w1s[0:RP1, g, r, 0:P], ident[0:RP1, 0:RP1])
                    t.transpose(t1b[:, c:c + RP1], w1s[0:RP1, g, r, C1:C], ident[0:RP1, 0:RP1])
                    last = t.transpose(t1b[0:C1, c:c + RP1], w1s[0:RP1, g, r, P:C], ident[0:RP1, 0:RP1])
            last.then_inc(prep_t, 1)
            for m in range(MT):
                for g in range(GROUPS):
                    last = t.transpose(t2[m][:, g, :], w2s[0:RP2, g, m, :], ident[0:RP2, 0:RP2])
            last.then_inc(prep_t, 1)
            pe.wait_ge(prep_done, 3 + 2 * GROUPS + MT)
            pe.wait_ge(ln[0]["lo"], TC)
            conv_phase(0, cadd, (None, 0), 0, TC)
            pe.wait_ge(ln[0]["lo"], TILES)
            conv_phase(1, cev, (cadd, QW), 1, 0)

            for g in range(2):
                pe.wait_ge(cev[g], QW)
            for s in range(-LEAD, FT + LAG2):
                u = s + LEAD + TC
                if u < TILES:
                    sums1(1, u, u % 2, u - TC)
                if TC < u <= TILES:
                    sums2(1, u - 1, (u - 1) % 2, last=(u == TILES))
                if s == 0:
                    pe.wait_ge(ld_wt, 16)
                if 0 <= s < FT:
                    pe.wait_ge(ld_ta[s % 2], 48 * (s // 2 + 1))
                    ta = TA[:, s % 2, :].rearrange("p (n e) -> p n e", e=2)
                    tb = TB[:, s % 2, 1:1 + 2 * HALF].rearrange("p (n e) -> p n e", e=2)
                    for m in range(MT):
                        c = s * MT + m
                        if c >= 4:
                            pe.wait_ge(ev1, c - 3)
                        o = m1p[c % 4][:, :]
                        fs = slice(m * P, (m + 1) * P)
                        t.matmul(o, W1A[:, fs], ta[:, :, 0], start=True, stop=False)
                        t.matmul(o, W1A[:, fs], ta[:, :, 1], start=False, stop=False)
                        t.matmul(o, W1B[:, fs], tb[:, :, 0], start=False, stop=True).then_inc(mm1, 1)
                u = s - LAG2
                if 0 <= u < FT:
                    if u == 0:
                        pe.wait_ge(ln[1]["sd"], TILES)
                    if u >= 2:
                        pe.wait_ge(ev2, 2 * (u - 1))
                    for m in range(MT):
                        if m % MH == 0:
                            pe.wait_ge(lo2, 2 * u + m // MH + 1)
                        for n, src in enumerate((HI[:, u % 2, m, :], low_half(u)[:, m, :])):
                            last = t.matmul(m2p[0][u % 2], W2T[:, m, 0:P], src, start=(m == n == 0),
                                            stop=(m == MT - 1 and n == 1))
                    last.then_inc(mm2[0], 1)
                    for m in range(MT):
                        for n, src in enumerate((HI[:, u % 2, m, :], low_half(u)[:, m, :])):
                            for e in range(2):
                                last = t.matmul(m2p[1][u % 2][e * C1:(e + 1) * C1, 0:QTR], W2T[:, m, P:C],
                                                src[:, e * QTR:(e + 1) * QTR], start=(m == n == 0),
                                                stop=(m == MT - 1 and n == 1))
                    last.then_inc(mm2[1], 1)


def kernel(x, L0_conv_weight, L0_ffn_W1, L0_ffn_b1, L0_ffn_W2, L0_ffn_b2):
    import numpy as np
    import concourse.bacc as bacc
    from concourse.bass_utils import run_bass_kernel_spmd

    nc = bacc.Bacc("TRN2", target_bir_lowering=False, num_devices=1)
    arrays, args = {}, []
    for name, a in (("x", np.asarray(x).reshape(B, C, PIX)), ("cw", L0_conv_weight), ("w1", L0_ffn_W1),
                    ("b1", L0_ffn_b1), ("w2", L0_ffn_W2), ("b2", L0_ffn_b2)):
        a = np.ascontiguousarray(a)
        arrays[name] = a
        args.append(nc.dram_tensor(name, a.shape, mybir.dt.from_np(a.dtype), kind="ExternalInput").ap())
    out = nc.dram_tensor("out", (B, C, PIX), F32, kind="ExternalOutput").ap()
    build(nc, *args, out)
    r = run_bass_kernel_spmd(nc, [arrays], core_ids=[0])
    return r.results[0]["out"].reshape(B, C, H, W)
```

```python
import concourse.bass as bass
from concourse import mybir
from contextlib import ExitStack

F32 = mybir.dt.float32
F16 = mybir.dt.float16
ALU = mybir.AluOpType
ACT = mybir.ActivationFunctionType
AX = mybir.AxisListType
RMAX = bass.bass_isa.ReduceOp.max

P = 128
B, C, H, W = 16, 192, 32, 32
PIX = H * W
HID = 4 * C
KS, PAD = 7, 3
GROUPS = 5
C1 = C - P
CHUNKS = (2, 3, 3)
FIRST = (0, CHUNKS[0], CHUNKS[0] + CHUNKS[1])
EARLY = 2 * CHUNKS[0]
KEPT = 2 * (CHUNKS[0] + CHUNKS[1])
QW = 32
HALF = PIX // 2
QTR = HALF // 2
HROWS = H // 2
TILES = B
JOBS = 2 * TILES
TW = 3 * HALF
NST = 3 * HROWS
DEV = 4
CUN = 4
UNITS = 32 // CUN
SLOT0 = (2 * CHUNKS[0] + 3, 2 * (CHUNKS[0] + CHUNKS[1]) + 3, TILES + 2 * CHUNKS[0])
SLOTF = TILES + 2 * (CHUNKS[0] + CHUNKS[1])
WITH = tuple(z - a for a, z in zip(SLOT0, SLOT0[1:] + (SLOTF,)))
PW = 3 * PIX
XSC, WSC = 16.0, 256.0
QB, QEPS = 128.0, 1e-5
CLIP = 127.99999237060547
HSC = 256.0
MT = HID // P
MH = MT // 2
RP1 = HID // GROUPS // 3
RP2 = C // GROUPS
FT = (B // GROUPS * GROUPS) * 2
GT = FT // GROUPS
LAST = FT - GT
OW = HALF + QTR
YR, Y2R = 8, 8
LAGA = GT
LAG2 = LAGA + 1
LAGE = LAG2 + 1
LAGF = LAGE + GT
LEAD = 2
RW = 64
PREP = 3 + 2 + MT
KP = 2 * KS


def build(nc, x, cw, w1, b1, w2, b2, out):
    ctx = ExitStack()
    with ctx:
        arena = ctx.enter_context(nc.sbuf_tensor("arena", [P, 51712], F32))

        def view(at, words, dt=F32):
            v = arena[:, at:at + words]
            return v if dt == F32 else v.bitcast(dt)

        def sb(name, shape, dt=F32):
            return ctx.enter_context(nc.sbuf_tensor(name, shape, dt))

        def sem(name):
            return ctx.enter_context(nc.semaphore(name))

        ker_d = nc.dram_tensor("ker_d", (C // 2, RW, 2 * KP), F16).ap()
        band_d = nc.dram_tensor("band_d", (C // 2, QW, QW * 2 * KP), F16).ap()
        wt_d = nc.dram_tensor("wt_d", (P, 2 * HID + MT * C), F16).ap()
        x1_d = nc.dram_tensor("x1_d", (B, C, PIX), F32).ap()
        tn_d = nc.dram_tensor("tn_d", (B, C, PIX), F32).ap()

        R0 = DEV * TW
        R1 = R0 + CHUNKS[0] * PW
        R3 = R1 + CHUNKS[1] * PW
        R2 = R3 + max(CHUNKS[0], CHUNKS[2]) * PW
        A2 = R2 + max(CHUNKS[1:]) * PW
        WP = R3 + CHUNKS[0] * PW
        A3 = A2 + 2 * 2 * 2 * QW * 4 * KP // 2
        assert A3 + 3 * TW == 51712

        def split_pairs(at, pairs):
            return [view(at + e * pairs * PW // 2, pairs * PW // 2, F16)
                    .rearrange("p (k s h i) -> p k s h i", k=pairs, s=3, h=H) for e in range(2)]

        XC = [view(a, k * PW).rearrange("p (k s n) -> p k s n", k=k, s=3)
              for a, k in zip((R0, R1, R2), CHUNKS)]
        XN = [split_pairs(a, k) for a, k in zip((R3, R2, R3), CHUNKS)]
        BD = view(A2, A3 - A2, F16).rearrange("p (g r c j k) -> p g r c j k", g=2, r=2, c=P, j=2)
        STG = view(A3, 3 * TW).rearrange("p (r s n) -> p r s n", r=3, s=3)
        DV = view(0, DEV * TW).rearrange("p (r s n) -> p r s n", r=DEV, s=3)
        w1f = view(WP, GROUPS * 3 * C).rearrange("p (g n) -> p g n", g=GROUPS)
        at = WP + GROUPS * 3 * C
        w1s = view(at, GROUPS * 3 * C // 2, F16).rearrange("p (g r c) -> p g r c", g=GROUPS, r=3)
        at += GROUPS * 3 * C // 2
        w2f = view(at, GROUPS * HID).rearrange("p (g n) -> p g n", g=GROUPS)
        at += GROUPS * HID
        w2s = view(at, GROUPS * HID // 2, F16).rearrange("p (g m f) -> p g m f", g=GROUPS, m=MT)
        at += GROUPS * HID // 2
        kraw = view(at, 98)[0:C // 2].rearrange("p (s a b) -> p s a b", s=2, a=KS)
        kacc = view(at + 98, 98)[0:C // 2].rearrange("p (s a b) -> p s a b", s=2, a=KS)
        kpad = view(at + 196, 896, F16)[0:C // 2].rearrange("p (t s k) -> p t s k", t=RW, s=2)
        ones = view(at + 1092, P)
        assert at + 1220 <= A2
        WTN = 2 * HID + MT * C
        at = A2

        def weights(v):
            return (v[:, 0:HID], v[:, HID:2 * HID], v[:, 2 * HID:WTN].rearrange("p (m c) -> p m c", m=MT))
        wtb = view(WP, WTN // 2, F16)
        W1P, W1Q, W2P = weights(wtb)
        TAW = view(at, 2 * HALF).rearrange("p (r n) -> p r n", r=2)
        TA = view(at, 2 * HALF, F16).rearrange("p (r n) -> p r n", r=2)
        at += 2 * HALF
        TB = view(at, 2 * (HALF + 1), F16).rearrange("p (r n) -> p r n", r=2)
        at += 2 * (HALF + 1) + 2
        HI = view(at, MT * HALF, F16).rearrange("p (r m n) -> p r m n", r=2, m=MT)
        at += MT * HALF
        WT = view(at, WTN // 2, F16)
        W1A, W1B, W2T = weights(WT)
        at += WTN // 2
        assert at <= A3
        Y = view(R0, YR * MT * HALF).rearrange("p (r m n) -> p r m n", r=YR, m=MT)
        assert R0 + YR * MT * HALF == R2
        Y2 = view(R2, Y2R * OW).rearrange("p (r n) -> p r n", r=Y2R)
        XO = view(R2 + Y2R * OW, 2 * OW).rearrange("p (r n) -> p r n", r=2)
        assert (Y2R + 2) * OW <= A2 - R2

        XE = view(R0, EARLY * TW).rearrange("p (r s n) -> p r s n", r=EARLY, s=3)
        assert LAST % YR == 0 and GT == YR - 2 and GT * OW <= 2 * MT * HALF
        SPARE = view(R0, GT * OW).rearrange("p (r n) -> p r n", r=GT)

        sumlo = sb("sumlo", [P, P])
        sumhi = sb("sumhi", [P, P])
        sumall = sb("sumall", [P, P])
        ident = sb("ident", [P, P], F16)
        b1s = sb("b1s", [P, MT])
        b2s = sb("b2s", [P, 2])
        eps = sb("eps", [P, 2])
        S1 = sb("S1", [P, 2, NST])
        S2 = sb("S2", [P, 2, NST])
        MU = sb("MU", [P, 2, NST])
        SD = sb("SD", [P, 2, NST])
        RS = sb("RS", [P, 2, NST])
        wsum = sb("wsum", [P, 2 * GROUPS])
        wmean = sb("wmean", [P, 2 * GROUPS])
        am = sb("am", [P, GT])
        am2 = sb("am2", [P, GT])
        gm = sb("gm", [P, 8])

        bank = [ctx.enter_context(nc.psum_tensor(f"bank{i}", [P, 512], F32)) for i in range(5)]
        sqp = ctx.enter_context(nc.psum_tensor("sqp", [P, TW], F32))
        cps = bank[0:4]
        stp = bank[4]
        m1p = bank[0:4]
        m2p = [[bank[4][:, :], sqp[:, 0:512]], [sqp[:, 512:1024], sqp[:, 1024:1536]]]
        t1a = bank[0][:, 0:480].bitcast(F16)
        t1b = bank[1][:, 0:480].bitcast(F16)
        t2 = [bank[2 + m // 3][:, (m % 3) * 96:(m % 3) * 96 + 95].bitcast(F16).rearrange("p (g q) -> p g q", g=GROUPS)
              for m in range(MT)]

        ld_w = sem("ld_w"); ld_k = sem("ld_k"); ld_b = sem("ld_b")
        ld_x = [sem(f"ld_x{i}") for i in range(3)]
        ld_band = [sem(f"ld_band{r}") for r in range(2)]
        st_ker = sem("st_ker"); st_band = sem("st_band"); st_wt = sem("st_wt"); ld_wt = sem("ld_wt")
        st_x1 = sem("st_x1"); st_tn = sem("st_tn")
        consts = sem("consts"); zeroed = sem("zeroed")
        ker_step = sem("ker_step"); bias_step = sem("bias_step")
        prep_sum = sem("prep_sum"); prep_tot = sem("prep_tot"); prep_mean = sem("prep_mean")
        prep_sign = sem("prep_sign"); prep_t = sem("prep_t"); prep_done = sem("prep_done")
        ln = {n: sem(f"ln_{n}") for n in "s1 mps mu d sq s2 vps sd r xn hi lo".split()}
        xb = sem("xb")
        xadd = sem("xadd")
        xt = sem("xt")
        tt = sem("tt")
        conv = sem("conv")
        free = [sem(f"free{i}") for i in range(4)]
        ld_ta = [sem(f"ld_ta{i}") for i in range(2)]
        ld_xo = [sem(f"ld_xo{i}") for i in range(2)]
        ld_xl = sem("ld_xl")
        st_o = [sem(f"st_o{i}") for i in range(2)]
        st_tail = sem("st_tail")
        mm1 = sem("mm1"); ev1 = sem("ev1"); amx = sem("amx")
        gmx = sem("gmx"); gall = sem("gall"); gsc_t = sem("gsc_t"); gsc = sem("gsc")
        gelu = sem("gelu"); hs = sem("hs"); hi2 = sem("hi2"); lo2 = sem("lo2"); lo2v = sem("lo2v")
        mm2 = [sem("mm2a"), sem("mm2b")]; ev2 = sem("ev2"); amx2 = sem("amx2")
        gmx2 = sem("gmx2"); gall2 = sem("gall2"); gsc2_t = sem("gsc2_t"); gsc2 = sem("gsc2")
        clipd = sem("clipd"); fin = sem("fin")

        block = ctx.enter_context(nc.Block())

        def xslab(t, dram):
            k, cols = t // 2, slice((t % 2) * HALF, (t % 2 + 1) * HALF)
            return (dram[2 * k:2 * k + 2, 0:P, cols].rearrange("b c n -> c b n"),
                    dram[2 * k, P:C, cols], dram[2 * k + 1, P:C, cols])

        def load_x(eng, t, slot):
            a, lo, hi = xslab(t, x)
            eng.dma_start(STG[:, slot, 0:2, :], a).then_inc(ld_x[slot], 16)
            eng.dma_start(STG[0:C1, slot, 2, :], lo).then_inc(ld_x[slot], 16)
            eng.dma_start(STG[C1:P, slot, 2, :], hi).then_inc(ld_x[slot], 16)

        def store_tile(eng, t, dst, slot, done):
            a, lo, hi = xslab(t, dst)
            eng.dma_start(a, STG[:, slot, 0:2, :]).then_inc(done, 16)
            eng.dma_start(lo, STG[0:C1, slot, 2, :]).then_inc(done, 16)
            eng.dma_start(hi, STG[C1:P, slot, 2, :]).then_inc(done, 16)

        def chunk_of(t):
            c = max(c for c in range(3) if t // 2 >= FIRST[c])
            return c, t // 2 - FIRST[c]

        def xtile(t):
            c, k = chunk_of(t)
            return XC[c][:, k, :, (t % 2) * HALF:(t % 2 + 1) * HALF]

        def dev(n):
            return DV[:, n % DEV]

        def source(n):
            return dev(n) if KEPT <= n < TILES else xtile(n % TILES)

        def brings(n):
            return n >= TILES + KEPT

        def brought(n):
            return n + 1 if n < TILES else n + 1 - KEPT

        def slot_free(eng, n):
            if n >= DEV:
                eng.wait_ge(ln["lo"], n - DEV + 1)

        def slot(n, stages, channel=None, after=()):
            for i, (stage, lag) in enumerate(stages):
                if 0 <= n - lag < JOBS:
                    stage(n - lag)
                for j in range(CUN):
                    if channel and after[j] == i:
                        channel(j)

        def part(n, e):
            if n < TILES:
                (c, k), h0 = chunk_of(n), (n % 2) * HROWS
                return XN[c][e][:, k, :, h0:h0 + HROWS, :]
            return xtile(n - TILES).bitcast(F16).rearrange("p s (h i e) -> p s h i e", i=QW, e=2)[:, :, :, :, e]

        def rows(v):
            return v.rearrange("p s (h i) -> p s h i", i=QW)

        def per_row(v, par):
            return v[:, par, :].rearrange("p (s h) -> p s h", s=3).unsqueeze(3).to_broadcast([P, 3, HROWS, QW])

        def channel(v, i):
            return v[:, :, :, :, i:i + 1] if isinstance(i, int) else v[:, :, :, :, bass.ds(i, 1)]

        def conv_words(g, chunk, i):
            ns, pairs = 2 - g, CHUNKS[chunk]
            at = 2 * g * pairs * H
            v = XC[chunk][:, :, 2 * g:2 * g + ns, :].rearrange("p k s (h i) -> p k s h i", i=QW)
            return channel(v, i).rearrange("p k s h o -> p k (s h o)"), \
                cps[i % CUN][:, at:at + pairs * ns * H].rearrange("p (k n) -> p k n", k=pairs)

        def place(u):
            return YR - 1 - u % YR

        def low_half(u):
            return Y[:, place(u), :, :].bitcast(F16).rearrange("p m (n e) -> p m n e", e=2)[:, :, :, 0]

        def low_parts(u):
            if u < LAST:
                return (slice(0, MH), slice(MH, MT)), None
            return (slice(0, 2), slice(2, 4)), slice(4, MT)

        def result(u):
            if u < LAST:
                return XO[:, u % 2, :]
            return SPARE[:, u - LAST, :]

        def halves(dram, b, cols):
            return [dram[b, P:C, cols.start + e * QTR:cols.start + (e + 1) * QTR] for e in range(2)]

        def next_x(eng, n):
            if SLOTF + EARLY < n + 1 < JOBS:
                eng.wait_ge(xb, brought(n))
                load_x(eng, n + 1 - TILES, 2)

        def results(eng, n):
            if TILES <= n < JOBS:
                eng.wait_ge(xt, n - TILES + 1)
                store_tile(eng, n - TILES, x1_d, 0, st_x1)
            if TILES <= n - 4 < JOBS:
                eng.wait_ge(tt, n - TILES - 3)
                store_tile(eng, n - TILES - 4, tn_d, 1, st_tn)

        @block.sync
        def _(sp):
            sp.dma_start(kraw, cw.rearrange("(p s) o a b -> p (s o) a b", s=2)).then_inc(ld_k, 16)
            for t in range(3):
                load_x(sp, t, t)
            sp.wait_ge(ker_step, 12)
            sp.dma_start(ker_d, kpad.rearrange("p t s k -> p t (s k)")).then_inc(st_ker, 16)
            for g in range(GROUPS):
                sp.dma_start(w1f[0:RP1, g, :], w1[g * 3 * RP1:(g + 1) * 3 * RP1, :]
                             .rearrange("(p r) c -> p (r c)", r=3)).then_inc(ld_w, 16)
                sp.dma_start(w2f[0:RP2, g, :], w2[g * RP2:(g + 1) * RP2, :]).then_inc(ld_w, 16)
            sp.wait_ge(st_ker, 16)
            for n in range(4):
                m0, mn, step = n * (C // 8), C // 8, 2 * KP
                src = bass.AP(ker_d.tensor, (m0 * RW + QW - 1) * step, [[RW * step, mn], [-step, QW], [1, QW * step]])
                sp.dma_start(band_d[m0:m0 + mn, :, :], src).then_inc(st_band, 16)
            sp.dma_start(b1s[:, :], b1.rearrange("(m p) -> p m", p=P), allow_slow_non_contiguous=True).then_inc(ld_b, 16)
            sp.dma_start(b2s[:, 0:1], b2[0:P].rearrange("(p o) -> p o", o=1)).then_inc(ld_b, 16)
            for e in range(2):
                sp.dma_start(b2s[e * C1:(e + 1) * C1, 1:2], b2[P:C].rearrange("(p o) -> p o", o=1)).then_inc(ld_b, 16)

            for t in range(3, SLOT0[0] + 2):
                sp.wait_ge(xb, t - 2)
                load_x(sp, t, t % 3)
            sp.wait_ge(st_band, 64)
            sp.wait_ge(zeroed, 1)

            def load_bands(pair, r, done):
                if done is not None:
                    sp.wait_ge(conv, done)
                for q in range(4):
                    quads = band_d.rearrange("(q m) w n -> q m w n", q=C // QW)[q::4 + q % 2 - q]
                    at = slice(pair, pair + 1) if isinstance(pair, int) else bass.ds(pair, 1)
                    src = quads[0:2, at, :, :].rearrange("g o w n -> w (g o) n")
                    dst = BD[q * QW:(q + 1) * QW, :, r, q * QW:(q + 1) * QW, :, :].rearrange("p g c j k -> p g (c j k)")
                    sp.dma_start(dst, src).then_inc(ld_band[r], 16)

            for r in range(2):
                load_bands(r, r, None)
            for chunk in range(3):
                with sp.Fori(1 if chunk == 0 else 0, UNITS) as m:
                    for r in range(2):
                        load_bands(2 * m + r, r, 4 * m + 2 * r - 2 + 32 * chunk)

            def load_tokens(s):
                b, half, cols = s // 2, s % 2, slice((s % 2) * HALF, (s % 2 + 1) * HALF)
                sp.wait_ge(st_tn, 48 * (b // 2 * 2 + half + 1))
                if s >= 2:
                    sp.wait_ge(mm1, MT * (s - 1))
                sp.dma_start(TAW[:, s % 2, :], tn_d[b, 0:P, cols]).then_inc(ld_ta[s % 2], 16)
                src = tn_d[b, P:C, cols].bitcast(F16)
                sp.dma_start(TB[0:C1, s % 2, 1:1 + 2 * HALF], src).then_inc(ld_ta[s % 2], 16)
                sp.dma_start(TB[C1:P, s % 2, 0:2 * HALF], src).then_inc(ld_ta[s % 2], 16)

            def load_x1(u):
                b, half, cols = u // 2, u % 2, slice((u % 2) * HALF, (u % 2 + 1) * HALF)
                sp.wait_ge(st_x1, 48 * (b // 2 * 2 + half + 1))
                if u >= 2:
                    sp.wait_ge(st_o[u % 2], 48 * (u // 2))
                sp.dma_start(result(u)[:, 0:HALF], x1_d[b, 0:P, cols]).then_inc(ld_xo[u % 2], 16)
                for e, src in enumerate(halves(x1_d, b, cols)):
                    sp.dma_start(result(u)[e * C1:(e + 1) * C1, HALF:OW], src).then_inc(ld_xo[u % 2], 16)

            def store(u):
                b, cols = u // 2, slice((u % 2) * HALF, (u % 2 + 1) * HALF)
                sp.wait_ge(fin, u + 1)
                sp.dma_start(out[b, 0:P, cols], result(u)[:, 0:HALF]).then_inc(st_o[u % 2], 16)
                for e, dst in enumerate(halves(out, b, cols)):
                    sp.dma_start(dst, result(u)[e * C1:(e + 1) * C1, HALF:OW]).then_inc(st_o[u % 2], 16)

            def image(u, dram):
                two, b = SPARE[:, u - LAST:u - LAST + 2, :], u // 2
                upper = dram[b, P:C, :].rearrange("c (t e n) -> c t e n", t=2, e=2)
                return [(two[:, :, 0:HALF], dram[b, 0:P, :].rearrange("c (t n) -> c t n", t=2))] + \
                    [(two[e * C1:(e + 1) * C1, :, HALF:OW], upper[:, :, e, :]) for e in range(2)]

            sp.wait_ge(conv, 3 * QW)
            sp.wait_ge(st_wt, 16)
            sp.dma_start(WT, wt_d[:, :]).then_inc(ld_wt, 16)
            for s in range(-LEAD, FT + LAGF + 1):
                n = SLOTF + LEAD + s
                next_x(sp, n)
                results(sp, n)
                if 0 <= s + 2 < FT:
                    load_tokens(s + 2)
                u = s - LAGF - 1
                if 0 <= u < LAST:
                    store(u)
                if LAST <= u < FT and u % 2:
                    sp.wait_ge(fin, u + 1)
                    for here, dst in image(u - 1, out):
                        sp.dma_start(dst, here).then_inc(st_tail, 16)
                if s == LAST + LAG2 + 1:
                    sp.wait_ge(mm2[1], LAST)
                    for u in range(LAST, FT, 2):
                        for here, src in image(u, x1_d):
                            sp.dma_start(here, src).then_inc(ld_xl, 16)
                if 0 <= s - LAGF + 1 < LAST:
                    if s - LAGF + 1 == 0:
                        sp.wait_ge(tt, TILES)
                    load_x1(s - LAGF + 1)
                if s == LAGF:
                    sp.wait_ge(st_x1, 48 * TILES)
                    sp.dma_start(out[B - 1, :, :], x1_d[B - 1, :, :]).then_inc(st_tail, 16)
            sp.wait_ge(st_tail, 16 + 24 * GT)
            for e in range(2):
                sp.wait_ge(st_o[e], 48 * (LAST // 2))
            sp.wait_ge(st_tn, 48 * TILES)

        @block.gpsimd
        def _(pool):
            pool.memset(ident[:, :], 0.0).then_inc(consts, 1)
            pool.memset(sumlo[:, :], 0.0).then_inc(consts, 1)
            pool.memset(sumhi[:, :], 0.0).then_inc(consts, 1)
            pool.memset(sumall[:, :], 0.0).then_inc(consts, 1)
            pool.memset(ones, 1.0).then_inc(consts, 1)
            pool.memset(eps[:, 0:1], 1e-6 / (XSC * XSC)).then_inc(consts, 1)
            pool.memset(eps[:, 1:2], 1e-5 / (XSC * XSC)).then_inc(consts, 1)
            n = 7
            pool.wait_ge(consts, n)
            pool.affine_select(out=ident[:, :], in_=ident[:, :], compare_op=ALU.not_equal, fill=1.0, base=0,
                               pattern=[[-1, P]], channel_multiplier=1).then_inc(consts, 1)
            n += 1
            for q in range(4):
                for m in (sumall, sumlo if q < 2 else sumhi):
                    v = m[:, :].rearrange("p (a b) -> p a b", b=QW)
                    pool.affine_select(out=v, in_=v, compare_op=ALU.not_equal, fill=1.0, base=-q * QW,
                                       pattern=[[0, 4], [-1, QW]], channel_multiplier=1).then_inc(consts, 1)
                    n += 1
                    pool.wait_ge(consts, n)

            pool.memset(view(A2, A3 - A2), 0.0).then_inc(zeroed, 1)

            def centre(n):
                pool.wait_ge(ln["mu"], n + 1)
                slot_free(pool, n)
                pool.tensor_tensor(out=rows(dev(n)), in0=rows(source(n)), in1=per_row(MU, n % 2),
                                   op=ALU.subtract).then_inc(ln["d"], 1)

            def scale(n):
                pool.wait_ge(ln["r"], n + 1)
                v = rows(dev(n))
                pool.tensor_tensor(out=v, in0=v, in1=per_row(RS, n % 2), op=ALU.mult).then_inc(ln["xn"], 1)

            def low(n):
                if n >= TILES:
                    pool.wait_ge(ln["hi"], n + 1)
                    pool.tensor_tensor(out=part(n, 1), in0=rows(dev(n)), in1=part(n, 0),
                                       op=ALU.subtract).then_inc(ln["lo"], 1)

            stages = ((low, 3), (scale, 2), (centre, 0))
            for n in range(SLOTF):
                slot(n, stages)
            for s in range(-LEAD, FT + LAGF):
                slot(SLOTF + LEAD + s, stages)
                if 1 <= s <= FT and s % GT == 0:
                    g = s // GT - 1
                    pool.wait_ge(gmx, g + 1)
                    pool.partition_all_reduce(gm[:, 1:2], gm[:, 0:1], P, RMAX).then_inc(gall, 1)
                u = s - LAGA
                if 0 <= u < FT:
                    for e, ms in enumerate(low_parts(u)[0]):
                        pool.wait_ge(hi2, 2 * u + 1 + (ms.stop > MH))
                        pool.tensor_tensor(out=low_half(u)[:, ms, :], in0=Y[:, place(u), ms, :],
                                           in1=HI[:, u % 2, ms, :], op=ALU.subtract).then_inc(lo2, 1)
                u = s - LAGE
                if 0 <= u < FT and u % GT == GT - 1:
                    pool.wait_ge(gmx2, u // GT + 1)
                    pool.partition_all_reduce(gm[:, 5:6], gm[:, 4:5], P, RMAX).then_inc(gall2, 1)

        @block.scalar
        def _(act):
            def stat(dst, src, func, bias=None, **kw):
                def go(o, i, lo, hi):
                    b = {} if bias is None else {"bias": bias[lo:hi, :]}
                    return act.activation(o, i, func, **b, **kw)
                go(dst[:, 0:2 * HROWS], src[:, 0:2 * HROWS], 0, P)
                go(dst[0:C1, 2 * HROWS:NST], src[0:C1, 0:HROWS], 0, C1)
                return go(dst[C1:P, 2 * HROWS:NST], src[C1:P, HROWS:2 * HROWS], C1, P)

            def mean(n):
                act.wait_ge(ln["mps"], n + 1)
                stat(MU[:, n % 2, :], stp[:, (n % 2) * 32:(n % 2) * 32 + 32], ACT.Copy, scale=1.0 / C) \
                    .then_inc(ln["mu"], 1)

            def deviation(n):
                act.wait_ge(ln["vps"], n + 1)
                p = n // TILES
                stat(SD[:, n % 2, :], stp[:, 64 + (n % 2) * 32:96 + (n % 2) * 32], ACT.Sqrt,
                     bias=eps[:, p:p + 1], scale=1.0 / (C * XSC * XSC)).then_inc(ln["sd"], 1)

            def square(n):
                act.wait_ge(ln["d"], n + 1)
                if n >= 1:
                    act.wait_ge(ln["s2"], n)
                act.activation(sqp[:, :].rearrange("p (s n) -> p s n", s=3), dev(n), ACT.Square) \
                    .then_inc(ln["sq"], 1)

            def high(n):
                act.wait_ge(ln["xn"], n + 1)
                if n == 2 * CHUNKS[0]:
                    act.wait_ge(prep_done, PREP)
                if n == KEPT:
                    act.wait_ge(st_wt, 16)
                    act.wait_ge(conv, QW)
                if n >= TILES:
                    act.wait_ge(xt, n - TILES + 1)
                act.activation(part(n, 0), rows(dev(n)), ACT.Copy).then_inc(ln["hi"], 1)

            stages = ((deviation, 2), (high, 3), (square, 1), (mean, 0))

            def signs(g):
                act.activation(w1s[0:RP1, g, :, :], w1f[0:RP1, g, :].rearrange("p (r c) -> p r c", r=3), ACT.Sign,
                               bias=wmean[0:RP1, g:g + 1], scale=1.0).then_inc(prep_sign, 1)
                act.activation(w2s[0:RP2, g, :, :], w2f[0:RP2, g, :].rearrange("p (m f) -> p m f", m=MT), ACT.Sign,
                               bias=wmean[0:RP2, GROUPS + g:GROUPS + g + 1], scale=1.0).then_inc(prep_sign, 1)

            for n in range(SLOT0[0]):
                slot(n, stages)
                if n == 3:
                    act.wait_ge(prep_mean, 2)
                if 3 <= n < 6:
                    for g in range(2 * n - 6, min(2 * n - 4, GROUPS)):
                        signs(g)
            act.wait_ge(prep_done, PREP)
            act.dma_start(wt_d[:, :], wtb).then_inc(st_wt, 16)

            def fetch(n):
                if n + 2 < TILES:
                    act.wait_ge(xb, n)
                    load_x(act, n + 2, (n + 2) % 3)

            def keep(n):
                results(act, n)

            def evac(i):
                act.wait_ge(conv, 2 * QW + i + 1)
                for g in range(2):
                    dst, src = conv_words(g, 2, i)
                    act.activation(dst, src, ACT.Copy, scale=1.0 / (XSC * WSC)).then_inc(free[i % CUN], 1)

            stages = ((deviation, 2), (high, 3), (square, 1), (fetch, 0), (mean, 0), (keep, 0))
            for n in range(SLOT0[0], SLOT0[2]):
                slot(n, stages)
            early = {2: 0, 4: 1, 5: 2, 6: 3, 7: 4}
            for m in range(UNITS):
                def channel_of_unit(j):
                    if j == 1 and m in early:
                        act.wait_ge(xb, TILES + early[m])
                        load_x(act, KEPT + early[m], 2)
                    evac(CUN * m + j)

                if m < WITH[2]:
                    slot(SLOT0[2] + m, stages, channel_of_unit, (0, 2, 4, 5))
                else:
                    for j in range(CUN):
                        channel_of_unit(j)

            def hidden(s):
                for m in range(MT):
                    c = s * MT + m
                    act.wait_ge(mm1, c + 1)
                    if m == 0 and s == CHUNKS[2]:
                        act.wait_ge(tt, KEPT)
                    if m == 0 and s == CHUNKS[2] + CHUNKS[1]:
                        act.wait_ge(xt, KEPT + EARLY)
                    if m == 0 and s >= YR:
                        act.wait_ge(mm2[1], s - YR + 1)
                    act.activation(Y[:, place(s), m, :], m1p[c % 4][:, :], ACT.Identity, bias=b1s[:, m:m + 1],
                                   scale=1.0).then_inc(ev1, 1)

            def gelus(u):
                act.wait_ge(gsc, u // GT + 1)
                act.activation(Y[:, place(u), :, :], Y[:, place(u), :, :], ACT.Gelu, scale=gm[:, 3:4]).then_inc(gelu, 1)

            def highs(u):
                for e in range(2):
                    ms = slice(e * MH, (e + 1) * MH)
                    act.wait_ge(hs, 2 * u + e + 1)
                    if u >= 2:
                        act.wait_ge(mm2[1], u - 1)
                    act.activation(HI[:, u % 2, ms, :], Y[:, place(u), ms, :], ACT.Copy).then_inc(hi2, 1)

            stages = ((deviation, 2), (high, 3), (square, 1), (mean, 0))
            for s in range(-LEAD, FT + LAGF):
                slot(SLOTF + LEAD + s, stages)
                u = s - LAGA
                if 0 <= s < FT and (u < 0 or u % GT == 0):
                    hidden(s)
                if 0 <= u < FT - GT or u == FT - GT:
                    gelus(u)
                if 0 <= s < FT and not (u < 0 or u % GT == 0):
                    hidden(s)
                if FT - GT <= u < FT - 1:
                    gelus(u + 1)
                if 0 <= u < FT:
                    highs(u)

        @block.vector
        def _(dve):
            v = nc.vector
            v.memset(kpad, 0.0).then_inc(ker_step, 1)
            dve.wait_ge(ld_k, 16)
            rev = slice(None, None, -1)

            def rot(s, k):
                w = kraw[:, s, :, :]
                if k == 1:
                    return w[:, :, rev].rearrange("p a b -> p b a")
                if k == 2:
                    return w[:, rev, rev]
                return w[:, rev, :].rearrange("p a b -> p b a")
            n = 1
            for k in (1, 2, 3):
                for s in range(2):
                    v.tensor_tensor(out=kacc[:, s, :, :], in0=(kraw if k == 1 else kacc)[:, s, :, :], in1=rot(s, k),
                                    op=ALU.add).then_inc(ker_step, 1)
                n += 2
                dve.wait_ge(ker_step, n)
            v.tensor_scalar(kacc, kacc, 0.25 * WSC, None, ALU.mult).then_inc(ker_step, 1)
            dve.wait_ge(ker_step, 8)
            kr = kpad.rearrange("p t s (a e) -> p s t a e", e=2)
            t0 = QW - PAD - 1
            ends = [(kacc[:, s, :, :].rearrange("p a b -> p b a")[:, rev, :],
                     kr[:, s, t0:t0 + KS, :, 0], kr[:, s, t0:t0 + KS, :, 1]) for s in range(2)]
            for src, high, low in ends:
                v.tensor_copy(high, src).then_inc(ker_step, 1)
            dve.wait_ge(ker_step, 10)
            for src, high, low in ends:
                v.tensor_tensor(out=low, in0=src, in1=high, op=ALU.subtract).then_inc(ker_step, 1)

            def weight_sums():
                dve.wait_ge(ld_w, 160)
                v.memset(wsum[:, :], 0.0).then_inc(bias_step, 1)
                dve.wait_ge(bias_step, 1)
                v.reduce_sum(wsum[0:RP1, 0:GROUPS], w1f[0:RP1, :, :], axis=AX.X).then_inc(prep_sum, 1)
                v.reduce_sum(wsum[0:RP2, GROUPS:], w2f[0:RP2, :, :], axis=AX.X).then_inc(prep_sum, 1)

            def weight_means():
                dve.wait_ge(prep_tot, 1)
                v.tensor_scalar(wmean[:, 0:GROUPS], bank[0][:, 0:GROUPS], -1.0 / (3 * RP1 * C), None, ALU.mult) \
                    .then_inc(prep_mean, 1)
                v.tensor_scalar(wmean[:, GROUPS:], bank[0][:, GROUPS:2 * GROUPS], -1.0 / (RP2 * HID), None, ALU.mult) \
                    .then_inc(prep_mean, 1)
                dve.wait_ge(ld_b, 64)
                v.tensor_scalar(b1s[:, :], b1s[:, :], XSC, None, ALU.mult).then_inc(bias_step, 1)
                v.tensor_scalar(b2s[:, :], b2s[:, :], HSC, None, ALU.mult).then_inc(bias_step, 1)
                dve.wait_ge(bias_step, 3)

            def weight_copies():
                dve.wait_ge(prep_t, 1)
                v.memset(W1P[:, GROUPS * 3 * RP1:], 0.0).then_inc(prep_done, 1)
                v.memset(W1Q[:, GROUPS * 3 * RP1:], 0.0).then_inc(prep_done, 1)
                v.memset(W2P[:, :, GROUPS * RP2:], 0.0).then_inc(prep_done, 1)
                for dst, src in ((W1P, t1a), (W1Q, t1b)):
                    o = dst[:, 0:GROUPS * 3 * RP1].rearrange("p (g q r) -> p g r q", g=GROUPS, r=3)
                    i = src.rearrange("p (g r q) -> p g r q", g=GROUPS, r=3)[:, :, :, 0:RP1]
                    v.tensor_copy(o, i).then_inc(prep_done, 1)
                dve.wait_ge(prep_t, 2)
                for m in range(MT):
                    v.tensor_copy(W2P[:, m, 0:GROUPS * RP2].rearrange("p (g q) -> p g q", g=GROUPS),
                                  t2[m]).then_inc(prep_done, 1)

            def bring(n):
                if n < TILES:
                    dve.wait_ge(ld_x[n % 3], 48 * (n // 3 + 1))
                    if n >= KEPT:
                        slot_free(dve, n)
                    v.transpose(source(n), STG[:, n % 3, :, :]).then_inc(xb, 1)
                    dve.wait_ge(xb, n + 1)
                elif brings(n):
                    added = n - TILES - KEPT + 1
                    if n < SLOTF + EARLY:
                        xs = XE[:, n - SLOTF]
                    else:
                        xs = dev(n)
                        dve.wait_ge(ld_x[2], 48 * (TILES // 3 + added))
                        slot_free(dve, n)
                        v.transpose(xs, STG[:, 2, :, :]).then_inc(xb, 1)
                    dve.wait_ge(xb, brought(n))
                    if n == TILES + KEPT:
                        for f in free:
                            dve.wait_ge(f, 2 * UNITS * (chunk_of(n - TILES)[0] + 1))
                    x1 = xtile(n - TILES)
                    v.tensor_tensor(out=x1, in0=x1, in1=xs, op=ALU.add).then_inc(xadd, 1)
                    dve.wait_ge(xadd, added)

            def early(n):
                dve.wait_ge(ld_x[2], 48 * (TILES // 3 + n - SLOTF + 1))
                dve.wait_ge(tt, 2 * CHUNKS[0])
                v.transpose(XE[:, n - SLOTF], STG[:, 2, :, :]).then_inc(xb, 1)

            def red1(n):
                if n in (TILES, TILES + 2 * CHUNKS[0]):
                    for f in free:
                        dve.wait_ge(f, 2 * UNITS * (chunk_of(n - TILES)[0] + 1))
                v.reduce_sum(S1[:, n % 2, :].rearrange("p (s h) -> p s h", s=3), rows(source(n)), axis=AX.X) \
                    .then_inc(ln["s1"], 1)
                if n >= TILES:
                    if n > TILES:
                        dve.wait_ge(st_x1, 48 * (n - TILES))
                    v.transpose(STG[:, 0, :, :], xtile(n - TILES)).then_inc(xt, 1)

            def red2(n):
                dve.wait_ge(ln["sq"], n + 1)
                v.reduce_sum(S2[:, n % 2, :], sqp[:, :].rearrange("p (a i) -> p a i", i=QW), axis=AX.X) \
                    .then_inc(ln["s2"], 1)

            def recip(n):
                dve.wait_ge(ln["sd"], n + 1)
                v.reciprocal(RS[:, n % 2, :], SD[:, n % 2, :]).then_inc(ln["r"], 1)

            def low(n):
                if n < TILES:
                    dve.wait_ge(ln["hi"], n + 1)
                    v.tensor_tensor(out=part(n, 1), in0=rows(dev(n)), in1=part(n, 0),
                                    op=ALU.subtract).then_inc(ln["lo"], 1)

            def back(n):
                if n >= TILES:
                    dve.wait_ge(ln["lo"], n + 1)
                    if n > TILES:
                        dve.wait_ge(st_tn, 48 * (n - TILES))
                    v.transpose(STG[:, 1, :, :], xtile(n - TILES)).then_inc(tt, 1)

            stages = ((bring, 0), (red1, 0), (back, 4), (low, 3), (recip, 2), (red2, 1))

            def add_conv(chunk, i):
                dve.wait_ge(conv, QW * chunk + i + 1)
                for g in range(2):
                    xs, ps = conv_words(g, chunk, i)
                    v.scalar_tensor_tensor(out=xs, in0=ps, scalar=1.0 / (XSC * WSC), in1=xs, op0=ALU.mult,
                                           op1=ALU.add).then_inc(free[i % CUN], 1)

            for n in range(SLOT0[0]):
                slot(n, stages)
                if n == 1:
                    weight_sums()
                if n == 2:
                    weight_means()
            weight_copies()
            def add_lagging(chunk, c):
                if c >= 2:
                    add_conv(chunk, c - 2)

            for chunk in (0, 1):
                for m in range(UNITS):
                    if m < WITH[chunk]:
                        slot(SLOT0[chunk] + m, stages, lambda j: add_lagging(chunk, CUN * m + j), (0, 1, 3, 4))
                    else:
                        for j in range(CUN):
                            add_lagging(chunk, CUN * m + j)
                for i in range(QW - 2, QW):
                    add_conv(chunk, i)
            for n in range(SLOT0[2], SLOTF):
                slot(n, stages)
                if n >= SLOTF - 3:
                    early(n + 3)
            early(SLOTF + EARLY - 1)

            def vector_low(u):
                ms = low_parts(u)[1]
                dve.wait_ge(hi2, 2 * u + 2)
                v.tensor_tensor(out=low_half(u)[:, ms, :], in0=Y[:, place(u), ms, :], in1=HI[:, u % 2, ms, :],
                                op=ALU.subtract).then_inc(lo2v, 1)

            for s in range(-LEAD, FT + LAGF):
                slot(SLOTF + LEAD + s, stages)
                if 1 <= s <= FT:
                    u = s - 1
                    dve.wait_ge(ev1, MT * (u + 1))
                    v.tensor_reduce(am[:, u % GT:u % GT + 1], Y[:, place(u), :, :], AX.XY, ALU.max,
                                    apply_absolute_value=True).then_inc(amx, 1)
                    if u % GT == GT - 1:
                        g = u // GT + 1
                        dve.wait_ge(amx, s)
                        v.tensor_reduce(gm[:, 0:1], am[:, :], AX.X, ALU.max).then_inc(gmx, 1)
                        dve.wait_ge(gall, g)
                        v.tensor_scalar(gm[:, 2:3], gm[:, 1:2], 1.0 / XSC, QEPS, ALU.mult, ALU.add).then_inc(gsc_t, 1)
                        dve.wait_ge(gsc_t, 2 * g - 1)
                        v.reciprocal(gm[:, 2:3], gm[:, 2:3]).then_inc(gsc_t, 1)
                        dve.wait_ge(gsc_t, 2 * g)
                        if g >= 2:
                            dve.wait_ge(gelu, GT * (g - 1))
                        v.tensor_scalar(gm[:, 3:4], gm[:, 2:3], QB / XSC, None, ALU.mult).then_inc(gsc, 1)
                u = s - LAGA
                if 0 <= u < FT:
                    for e in range(2):
                        ms = slice(e * MH, (e + 1) * MH)
                        dve.wait_ge(gelu, u + 1)
                        v.tensor_scalar(Y[:, place(u), ms, :], Y[:, place(u), ms, :], HSC, HSC * CLIP, ALU.mult, ALU.min) \
                            .then_inc(hs, 1)
                u = s - LAGF
                if 0 <= u < FT and u % GT == 0:
                    g = u // GT + 1
                    dve.wait_ge(gall2, g)
                    v.tensor_scalar(gm[:, 6:7], gm[:, 5:6], 1.0 / HSC, QEPS, ALU.mult, ALU.add) \
                        .then_inc(gsc2_t, 1)
                    dve.wait_ge(gsc2_t, 2 * g - 1)
                    v.reciprocal(gm[:, 6:7], gm[:, 6:7]).then_inc(gsc2_t, 1)
                    dve.wait_ge(gsc2_t, 2 * g)
                    v.tensor_scalar(gm[:, 7:8], gm[:, 6:7], QB / HSC, None, ALU.mult).then_inc(gsc2, 1)
                if 0 <= u < FT:
                    dve.wait_ge(gsc2, u // GT + 1)
                    v.tensor_scalar(Y2[:, u % Y2R, :], Y2[:, u % Y2R, :], gm[:, 7:8], CLIP, ALU.mult, ALU.min) \
                        .then_inc(clipd, 1)
                    if u < LAST:
                        dve.wait_ge(ld_xo[u % 2], 48 * (u // 2 + 1))
                    else:
                        dve.wait_ge(ld_xl, 24 * GT)
                    dve.wait_ge(clipd, u + 1)
                    v.scalar_tensor_tensor(out=result(u), in0=Y2[:, u % Y2R, :], scalar=-CLIP,
                                           in1=result(u), op0=ALU.max, op1=ALU.add).then_inc(fin, 1)
                u = s - LAGE
                if 0 <= u < FT:
                    if u == 0:
                        dve.wait_ge(tt, TILES)
                    if u >= Y2R:
                        dve.wait_ge(fin, u - Y2R + 1)
                    for e, cols in ((0, slice(0, HALF)), (1, slice(HALF, OW))):
                        dve.wait_ge(mm2[e], u + 1)
                        v.tensor_scalar(Y2[:, u % Y2R, cols], m2p[e][u % 2][:, 0:cols.stop - cols.start],
                                        b2s[:, e:e + 1], None, ALU.add).then_inc(ev2, 1)
                    dve.wait_ge(ev2, 2 * (u + 1))
                    v.tensor_reduce(am2[:, u % GT:u % GT + 1], Y2[:, u % Y2R, :], AX.X, ALU.max,
                                    apply_absolute_value=True).then_inc(amx2, 1)
                    if u % GT == GT - 1:
                        dve.wait_ge(amx2, u + 1)
                        v.tensor_reduce(gm[:, 4:5], am2[:, :], AX.X, ALU.max).then_inc(gmx2, 1)
                if LAST <= s - LAGA < FT:
                    vector_low(s - LAGA)

        @block.tensor
        def _(pe):
            t = nc.tensor

            def channel_sums(out0, s):
                for img, edge in ((0, sumlo), (1, sumhi)):
                    o = stp[:, out0 + img * HROWS:out0 + (img + 1) * HROWS]
                    t.matmul(o, sumall[:, :], s[:, img * HROWS:(img + 1) * HROWS], start=True, stop=False)
                    last = t.matmul(o, edge[:, :], s[:, 2 * HROWS:NST], start=False, stop=True)
                return last

            def sums1(n, par):
                pe.wait_ge(ln["s1"], n + 1)
                channel_sums(par * 32, S1[:, par, :]).then_inc(ln["mps"], 1)

            def sums2(n, par):
                pe.wait_ge(ln["s2"], n + 1)
                channel_sums(64 + par * 32, S2[:, par, :]).then_inc(ln["vps"], 1)

            def stage2(n):
                if n + 1 < JOBS:
                    pe.wait_ge(ln["mu"], n + 2)
                else:
                    pe.wait_ge(ln["sd"], n)
                sums2(n, n % 2)

            def stage1(n):
                if n >= 2:
                    pe.wait_ge(ln["sd"], n - 1)
                elif n == 1:
                    pe.wait_ge(ln["mu"], 1)
                sums1(n, n % 2)

            stages = ((stage2, 2), (stage1, 0))

            def conv_channel(chunk, m, j4, first):
                j, r, i, pairs = j4 % 2, j4 // 2, CUN * m + j4, CHUNKS[chunk]
                if not first:
                    pe.wait_ge(free[j4], 2 * m + 2 * UNITS * chunk)
                pe.wait_ge(ld_band[r], 64 * m + 64 * (UNITS * chunk + 1))
                for g in range(2):
                    ns, at = 2 - g, 2 * g * pairs * H
                    ps = cps[j4][:, at:at + pairs * ns * H].rearrange("p (k s h) -> p k s h", k=pairs, s=ns)
                    order = [PAD] + [a for a in range(KS) if a != PAD]
                    for kh in order:
                        dh = kh - PAD
                        lo, hi = max(0, -dh), min(H, H - dh)
                        for wpart, xpart in ((0, 0), (0, 1), (1, 0)):
                            mv = channel(XN[chunk][xpart][:, :, 2 * g:2 * g + ns, lo + dh:hi + dh, :], i)
                            last = t.matmul(ps[:, :, :, lo:hi], BD[:, g, r, :, j, 2 * kh + wpart],
                                            mv.rearrange("p k s h o -> p k s (h o)"),
                                            start=(kh == PAD and wpart == xpart == 0),
                                            stop=(kh == order[-1] and wpart == 1))
                last.then_inc(conv, 1)

            def unit(chunk, m, parity=None, first=False):
                for j4 in range(CUN):
                    conv_channel(chunk, m, j4, first)
                    if parity is None:
                        continue
                    if j4 == 0:
                        pe.wait_ge(ln["mu"], m + SLOT0[chunk])
                        sums2(m + (SLOT0[chunk] - 2), parity)
                    if j4 == 2:
                        pe.wait_ge(ln["sd"], m + (SLOT0[chunk] - 1))
                        sums1(m + SLOT0[chunk], parity)

            pe.wait_ge(consts, 16)
            for n in range(SLOT0[0]):
                slot(n, stages)
                if n == 2:
                    pe.wait_ge(prep_sum, 2)
                    t.matmul(bank[0][:, 0:2 * GROUPS], ones, wsum[:, :], start=True, stop=True).then_inc(prep_tot, 1)
            pe.wait_ge(prep_sign, 2 * GROUPS)
            for g in range(GROUPS):
                for r in range(3):
                    c = (3 * g + r) * 64
                    t.transpose(t1a[:, c:c + RP1], w1s[0:RP1, g, r, 0:P], ident[0:RP1, 0:RP1])
                    t.transpose(t1b[:, c:c + RP1], w1s[0:RP1, g, r, C1:C], ident[0:RP1, 0:RP1])
                    last = t.transpose(t1b[0:C1, c:c + RP1], w1s[0:RP1, g, r, P:C], ident[0:RP1, 0:RP1])
            last.then_inc(prep_t, 1)
            for m in range(MT):
                for g in range(GROUPS):
                    last = t.transpose(t2[m][:, g, :], w2s[0:RP2, g, m, :], ident[0:RP2, 0:RP2])
            last.then_inc(prep_t, 1)
            pe.wait_ge(prep_done, PREP)
            for chunk in range(3):
                pe.wait_ge(ln["lo"], 2 * (FIRST[chunk] + CHUNKS[chunk]))
                par, have, m0 = SLOT0[chunk] % 2, WITH[chunk], 0
                if chunk == 0:
                    unit(0, 0, par, first=True)
                    m0 = 1
                with pe.Fori(m0, m0 + (have - m0) // 2) as h:
                    for e in range(2):
                        unit(chunk, 2 * h + (e - m0), (par + m0 + e) % 2)
                if (have - m0) % 2:
                    unit(chunk, have - 1, (par + have - 1) % 2)
                with pe.Fori(have, UNITS) as m:
                    unit(chunk, m)

            for f in free:
                pe.wait_ge(f, 3 * 2 * UNITS)
            for s in range(-LEAD, FT + LAG2):
                slot(SLOTF + LEAD + s, stages)
                if s == 0:
                    pe.wait_ge(ld_wt, 16)
                if 0 <= s < FT:
                    pe.wait_ge(ld_ta[s % 2], 48 * (s // 2 + 1))
                    ta = TA[:, s % 2, :].rearrange("p (n e) -> p n e", e=2)
                    tb = TB[:, s % 2, 1:1 + 2 * HALF].rearrange("p (n e) -> p n e", e=2)
                    for m in range(MT):
                        c = s * MT + m
                        if c >= 4:
                            pe.wait_ge(ev1, c - 3)
                        o = m1p[c % 4][:, :]
                        fs = slice(m * P, (m + 1) * P)
                        t.matmul(o, W1A[:, fs], ta[:, :, 0], start=True, stop=False)
                        t.matmul(o, W1A[:, fs], ta[:, :, 1], start=False, stop=False)
                        t.matmul(o, W1B[:, fs], tb[:, :, 0], start=False, stop=True).then_inc(mm1, 1)
                u = s - LAG2
                if 0 <= u < FT:
                    if u == 0:
                        pe.wait_ge(ln["sd"], JOBS)
                    if u >= 2:
                        pe.wait_ge(ev2, 2 * (u - 1))
                    ours, vectors = low_parts(u)
                    for m in range(MT):
                        for e, ms in enumerate(ours):
                            if m == ms.start:
                                pe.wait_ge(lo2, 2 * u + e + 1)
                        if vectors and m == vectors.start:
                            pe.wait_ge(lo2v, u - LAST + 1)
                        for n, src in enumerate((HI[:, u % 2, m, :], low_half(u)[:, m, :])):
                            last = t.matmul(m2p[0][u % 2], W2T[:, m, 0:P], src, start=(m == n == 0),
                                            stop=(m == MT - 1 and n == 1))
                    last.then_inc(mm2[0], 1)
                    for m in range(MT):
                        for n, src in enumerate((HI[:, u % 2, m, :], low_half(u)[:, m, :])):
                            for e in range(2):
                                last = t.matmul(m2p[1][u % 2][e * C1:(e + 1) * C1, 0:QTR], W2T[:, m, P:C],
                                                src[:, e * QTR:(e + 1) * QTR], start=(m == n == 0),
                                                stop=(m == MT - 1 and n == 1))
                    last.then_inc(mm2[1], 1)


def kernel(x, L0_conv_weight, L0_ffn_W1, L0_ffn_b1, L0_ffn_W2, L0_ffn_b2):
    import numpy as np
    import concourse.bacc as bacc
    from concourse.bass_utils import run_bass_kernel_spmd

    nc = bacc.Bacc("TRN2", target_bir_lowering=False, num_devices=1)
    arrays, args = {}, []
    for name, a in (("x", np.asarray(x).reshape(B, C, PIX)), ("cw", L0_conv_weight), ("w1", L0_ffn_W1),
                    ("b1", L0_ffn_b1), ("w2", L0_ffn_W2), ("b2", L0_ffn_b2)):
        a = np.ascontiguousarray(a)
        arrays[name] = a
        args.append(nc.dram_tensor(name, a.shape, mybir.dt.from_np(a.dtype), kind="ExternalInput").ap())
    out = nc.dram_tensor("out", (B, C, PIX), F32, kind="ExternalOutput").ap()
    build(nc, *args, out)
    r = run_bass_kernel_spmd(nc, [arrays], core_ids=[0])
    return r.results[0]["out"].reshape(B, C, H, W)
```
